# Optimizing a Trainium2 kernel written in Bass

```python
import numpy as np
import jax
import jax.numpy as jnp

def _softmax(x, axis=-1):
    return jax.nn.softmax(x, axis=axis)

def _gelu(x):
    return jax.nn.gelu(x, approximate=True)

def _silu(x):
    return jax.nn.silu(x)

def _sigmoid(x):
    return jax.nn.sigmoid(x)

def _layernorm(x, axis=-1, eps=1e-05):
    m = jnp.mean(x, axis=axis, keepdims=True)
    v = jnp.var(x, axis=axis, keepdims=True)
    return (x - m) / jnp.sqrt(v + eps)

def _scatter_add(tgt, idx, src, axis=0):
    return tgt.at[idx].add(src)

def _segment_sum(src, seg, n):
    return jax.ops.segment_sum(src, seg, n)
kernel_name = 'mk_cond_resid_d4_seqx_r2_0bb943'

def setup_inputs(seed: int=0):
    np.random.seed(seed)
    _w = jnp.asarray

    def _rec_inputs():
        import jax
        import jax.numpy as jnp
        _rk = jax.random.key(seed)
        x = 7.22e-05 + 1 * jax.random.normal(jax.random.fold_in(_rk, 1), (8, 512, 512), jnp.float32)
        _lenS = 512 - jax.random.randint(jax.random.fold_in(_rk, 7), (8,), 0, max(1, 512 // 4) + 1, jnp.int32)
        _lenS2 = 512 - jax.random.randint(jax.random.fold_in(_rk, 8), (8,), 0, max(1, 512 // 4) + 1, jnp.int32)
        fside_BxSxS_0 = 4.13588e-05 + 0.999923 * jax.random.normal(jax.random.fold_in(_rk, 11), (8, 512, 512), jnp.float32)
        itok_B_18_1004 = jax.random.randint(jax.random.fold_in(_rk, 12), (8,), 18, 1005, jnp.int32)
        itok_B_0_5 = jax.random.randint(jax.random.fold_in(_rk, 13), (8,), 0, 6, jnp.int32)
        itok_B_0_8 = jax.random.randint(jax.random.fold_in(_rk, 14), (8,), 0, 9, jnp.int32)
        itok_B_0_3 = jax.random.randint(jax.random.fold_in(_rk, 15), (8,), 0, 4, jnp.int32)
        return (x, fside_BxSxS_0, itok_B_18_1004, itok_B_0_5, itok_B_0_8, itok_B_0_3)
    x, fside_BxSxS_0, itok_B_18_1004, itok_B_0_5, itok_B_0_8, itok_B_0_3 = _rec_inputs()

    def _L0_cond_setup():
        import jax, jax.numpy as jnp
        import numpy as np
        B, L1, L2, DIN, DOUT, H = (8, 512, 512, 512, 512, 16)
        DH = DOUT // H
        SCALE = 1.0 / np.sqrt(DH).astype(np.float32)
        key = jax.random.key(seed)
        ks = jax.random.split(key, 13)
        s = 0.02
        return {'seq1': jax.random.normal(ks[0], (B, L1, DIN), jnp.float32), 'seq2': jax.random.normal(ks[1], (B, L2, DIN), jnp.float32), 'seq_len1': jax.random.randint(ks[2], (B,), 1, L1 + 1, jnp.int32), 'Wq': jax.random.normal(ks[3], (DIN, DOUT), jnp.float32) * s, 'bq': jnp.zeros((DOUT,), jnp.float32), 'Wk': jax.random.normal(ks[4], (DIN, DOUT), jnp.float32) * s, 'bk': jnp.zeros((DOUT,), jnp.float32), 'Wv': jax.random.normal(ks[5], (DIN, DOUT), jnp.float32) * s, 'bv': jnp.zeros((DOUT,), jnp.float32), 'Wo': jax.random.normal(ks[6], (DOUT, DOUT), jnp.float32) * s, 'bo': jnp.zeros((DOUT,), jnp.float32), 'b_prev': jax.random.normal(ks[7], (1, 1, DIN), jnp.float32) * s, 'b_self': jax.random.normal(ks[8], (1, 1, DIN), jnp.float32) * s}
    _L0_cond_all = _L0_cond_setup()
    _L0_cond_in = {k: v for k, v in _L0_cond_all.items() if k in ('Wq', 'bq', 'Wk', 'bk', 'Wv', 'bv', 'Wo', 'bo', 'b_prev', 'b_self')}
    del _L0_cond_all

    def _L1_cond_setup():
        import jax, jax.numpy as jnp
        import numpy as np
        B, S, D = (8, 512, 512)
        NUM_STAGES = 6
        key = jax.random.key(seed)
        k1, k2, k3, k4, k5 = jax.random.split(key, 5)
        return {'query': jax.random.normal(k1, (B, S, D), dtype=jnp.float32), 'key': jax.random.normal(k2, (B, S, D), dtype=jnp.float32), 'value': jax.random.normal(k3, (B, S, D), dtype=jnp.float32), 'braak_embed': jax.random.normal(k4, (NUM_STAGES, D), dtype=jnp.float32), 'braak_stages': jax.random.randint(k5, (B,), 0, NUM_STAGES, dtype=jnp.int64)}
    _L1_cond_all = _L1_cond_setup()
    _L1_cond_in = {k: v for k, v in _L1_cond_all.items() if k in ('braak_embed',)}
    del _L1_cond_all

    def _L2_cond_setup():
        import jax, jax.numpy as jnp
        import numpy as np
        LN_EPS = 1e-05
        key = jax.random.key(seed)
        ks = jax.random.split(key, 8)
        B, S, H, A, L = (32, 1024, 512, 128, 10)
        return {'hidden_states': jax.random.normal(ks[0], (B, S, H), dtype=jnp.float32), 'language_ids': jax.random.randint(ks[1], (B,), 0, L, dtype=jnp.int64), 'W1': jax.random.normal(ks[2], (L, H, A), dtype=jnp.float32) * (1.0 / np.sqrt(H)), 'b1': jnp.zeros((L, A), dtype=jnp.float32), 'W2': jax.random.normal(ks[3], (L, A, H), dtype=jnp.float32) * (1.0 / np.sqrt(A)), 'b2': jnp.zeros((L, H), dtype=jnp.float32), 'gamma': jnp.ones((L, H), dtype=jnp.float32), 'beta': jnp.zeros((L, H), dtype=jnp.float32)}
    _L2_cond_all = _L2_cond_setup()
    _L2_cond_in = {k: v for k, v in _L2_cond_all.items() if k in ('W1', 'b1', 'W2', 'b2', 'gamma', 'beta')}
    del _L2_cond_all

    def _L3_cond_setup():
        import jax, jax.numpy as jnp
        import numpy as np
        D = 512
        RANK = 16
        ALPHA = 16.0
        SCALING = ALPHA / RANK
        N_LANG = 4
        B, S = (32, 1024)
        key = jax.random.key(seed)
        k1, k2, k3, k4, k5 = jax.random.split(key, 5)
        x = jax.random.normal(k1, (B, S, D), dtype=jnp.float32)
        language_ids = jax.random.randint(k2, (B,), 0, N_LANG, dtype=jnp.int32)
        lora_A = jax.random.normal(k3, (N_LANG, RANK, D), dtype=jnp.float32) * 0.02
        lora_B = jax.random.normal(k4, (N_LANG, D, RANK), dtype=jnp.float32) * 0.02
        lang_embed = jax.random.normal(k5, (N_LANG, D), dtype=jnp.float32) * 0.02
        return {'x': x, 'language_ids': language_ids, 'lora_A': lora_A, 'lora_B': lora_B, 'lang_embed': lang_embed}
    _L3_cond_all = _L3_cond_setup()
    _L3_cond_in = {k: v for k, v in _L3_cond_all.items() if k in ('lora_A', 'lora_B', 'lang_embed')}
    del _L3_cond_all
    return {'x': x, 'fside_BxSxS_0': fside_BxSxS_0, 'itok_B_18_1004': itok_B_18_1004, 'itok_B_0_5': itok_B_0_5, 'itok_B_0_8': itok_B_0_8, 'itok_B_0_3': itok_B_0_3, 'L0_cond_Wq': _L0_cond_in['Wq'], 'L0_cond_bq': _L0_cond_in['bq'], 'L0_cond_Wk': _L0_cond_in['Wk'], 'L0_cond_bk': _L0_cond_in['bk'], 'L0_cond_Wv': _L0_cond_in['Wv'], 'L0_cond_bv': _L0_cond_in['bv'], 'L0_cond_Wo': _L0_cond_in['Wo'], 'L0_cond_bo': _L0_cond_in['bo'], 'L0_cond_b_prev': _L0_cond_in['b_prev'], 'L0_cond_b_self': _L0_cond_in['b_self'], 'L1_cond_braak_embed': _L1_cond_in['braak_embed'], 'L2_cond_W1': _L2_cond_in['W1'], 'L2_cond_b1': _L2_cond_in['b1'], 'L2_cond_W2': _L2_cond_in['W2'], 'L2_cond_b2': _L2_cond_in['b2'], 'L2_cond_gamma': _L2_cond_in['gamma'], 'L2_cond_beta': _L2_cond_in['beta'], 'L3_cond_lora_A': _L3_cond_in['lora_A'], 'L3_cond_lora_B': _L3_cond_in['lora_B'], 'L3_cond_lang_embed': _L3_cond_in['lang_embed']}

def reference(x, fside_BxSxS_0, itok_B_18_1004, itok_B_0_5, itok_B_0_8, itok_B_0_3, L0_cond_Wq, L0_cond_bq, L0_cond_Wk, L0_cond_bk, L0_cond_Wv, L0_cond_bv, L0_cond_Wo, L0_cond_bo, L0_cond_b_prev, L0_cond_b_self, L1_cond_braak_embed, L2_cond_W1, L2_cond_b1, L2_cond_W2, L2_cond_b2, L2_cond_gamma, L2_cond_beta, L3_cond_lora_A, L3_cond_lora_B, L3_cond_lang_embed):
    import jax
    import jax.numpy as jnp

    def _L0_cond_ref(seq1, seq2, seq_len1, Wq, bq, Wk, bk, Wv, bv, Wo, bo, b_prev, b_self):
        import jax, jax.numpy as jnp
        import numpy as np
        B, L1, L2, DIN, DOUT, H = (8, 512, 512, 512, 512, 16)
        DH = DOUT // H
        SCALE = 1.0 / np.sqrt(DH).astype(np.float32)
        b, l1, _ = seq1.shape
        l2 = seq2.shape[1]
        query = seq2 + b_self
        key = jnp.concatenate([seq1 + b_prev, seq2 + b_self], 1)
        value = jnp.concatenate([seq1, seq2], 1)
        q = (query @ Wq + bq).reshape(b, l2, H, DH).transpose(0, 2, 1, 3)
        k = (key @ Wk + bk).reshape(b, l1 + l2, H, DH).transpose(0, 2, 1, 3)
        v = (value @ Wv + bv).reshape(b, l1 + l2, H, DH).transpose(0, 2, 1, 3)
        score_prev = jnp.einsum('bhqd,bhkd->bhqk', q, k[:, :, :l1]) * SCALE
        score_self = (q * k[:, :, l1:]).sum(-1, keepdims=True) * SCALE
        mask = jnp.arange(l1)[None, :] < seq_len1[:, None]
        score_prev = jnp.where(mask[:, None, None, :], score_prev, -jnp.inf)
        score = jnp.concatenate([score_prev, score_self], -1)
        weights = jax.nn.softmax(score, axis=-1)
        attn = jnp.einsum('bhqk,bhkd->bhqd', weights[..., :-1], v[:, :, :l1])
        attn = attn + weights[..., -1:] * v[:, :, l1:]
        attn = attn.transpose(0, 2, 1, 3).reshape(b, l2, H * DH)
        return attn @ Wo + bo

    def _L1_cond_ref(query, key, value, braak_embed, braak_stages):
        import jax, jax.numpy as jnp
        import numpy as np
        B, S, D = (8, 512, 512)
        NUM_STAGES = 6
        bias = braak_embed[braak_stages][..., None]
        q = query + bias
        attn = jnp.einsum('bsd,btd->bst', q, key)
        attn = jax.nn.softmax(attn, axis=-1)
        return jnp.einsum('bst,btd->bsd', attn, value)

    def _L2_cond_ref(hidden_states, language_ids, W1, b1, W2, b2, gamma, beta):
        import jax, jax.numpy as jnp
        import numpy as np
        LN_EPS = 1e-05
        w1 = W1[language_ids]
        w2 = W2[language_ids]
        h = jnp.einsum('bsh,bha->bsa', hidden_states, w1) + b1[language_ids][:, None, :]
        h = jax.nn.relu(h)
        adapted = jnp.einsum('bsa,bah->bsh', h, w2) + b2[language_ids][:, None, :]
        x = hidden_states + adapted
        mean = jnp.mean(x, axis=-1, keepdims=True)
        var = jnp.mean(jnp.square(x - mean), axis=-1, keepdims=True)
        normed = (x - mean) * jax.lax.rsqrt(var + LN_EPS)
        return normed * gamma[language_ids][:, None, :] + beta[language_ids][:, None, :]

    def _L3_cond_ref(x, language_ids, lora_A, lora_B, lang_embed):
        import jax, jax.numpy as jnp
        import numpy as np
        D = 512
        RANK = 16
        ALPHA = 16.0
        SCALING = ALPHA / RANK
        N_LANG = 4
        B, S = (32, 1024)
        A = lora_A[language_ids]
        Bm = lora_B[language_ids]
        emb = lang_embed[language_ids]
        t = jnp.einsum('bsd,brd->bsr', x, A)
        lora_out = jnp.einsum('bsr,bdr->bsd', t, Bm) * SCALING
        return lora_out + emb[:, None, :]
    x = x + _L0_cond_ref(x, fside_BxSxS_0, itok_B_18_1004, L0_cond_Wq, L0_cond_bq, L0_cond_Wk, L0_cond_bk, L0_cond_Wv, L0_cond_bv, L0_cond_Wo, L0_cond_bo, L0_cond_b_prev, L0_cond_b_self)
    x = x + _L1_cond_ref(x, fside_BxSxS_0, fside_BxSxS_0, L1_cond_braak_embed, itok_B_0_5)
    x = x + _L2_cond_ref(x, itok_B_0_8, L2_cond_W1, L2_cond_b1, L2_cond_W2, L2_cond_b2, L2_cond_gamma, L2_cond_beta)
    x = x + _L3_cond_ref(x, itok_B_0_3, L3_cond_lora_A, L3_cond_lora_B, L3_cond_lang_embed)
    return x

_drawn_inputs = setup_inputs


def setup_inputs(seed=0):
    import zlib

    import numpy as np

    out = dict(_drawn_inputs(seed))
    spreads = {'L0_cond_bq': (0.0, 0.8),
     'L0_cond_bk': (0.0, 2.0),
     'L0_cond_bv': (0.0, 0.1),
     'L0_cond_bo': (0.0, 0.1),
     'L2_cond_b1': (0.0, 0.483),
     'L2_cond_b2': (0.0, 0.331),
     'L2_cond_gamma': (1.0, 0.2),
     'L2_cond_beta': (0.0, 0.1)}
    factors = {'L0_cond_Wq': 4.993,
     'L0_cond_Wk': 5.097,
     'L0_cond_b_prev': 38.753,
     'L0_cond_b_self': 8.0,
     'L3_cond_lang_embed': 6.759}
    for name, (base, spread) in spreads.items():
        noise = np.random.default_rng([zlib.crc32(name.encode()), seed]).standard_normal(out[name].shape)
        drawn = base * np.exp(spread * noise) if base else spread * noise
        out[name] = jnp.asarray(drawn.astype(out[name].dtype))
    for name, factor in factors.items():
        out[name] = (out[name] * factor).astype(out[name].dtype)
    return out
```

```python
from contextlib import ExitStack

import concourse.bass as bass
from concourse import mybir

F32 = mybir.dt.float32
F16 = mybir.dt.float16
I32 = mybir.dt.int32
ALU = mybir.AluOpType
ACT = mybir.ActivationFunctionType
AX_X = mybir.AxisListType.X

B, S, D = 8, 512, 512
H, DH = 16, 32
P = 128
NT = S // P
ND = D // P
NG, NJ = H // 4, 4
NSTEP = NG * NT
STAGES, LANGS, A, RLANGS, RANK = 6, 10, 128, 4, 16
SCALE = 1.0 / float(DH) ** 0.5
EPS = 1e-5
WS = 64.0
BIG = 32768.0
MASK_ROW = 3 * DH
SHIFT_ROW = MASK_ROW + 1
DMAS_PER_STACK = 2 * 3 * NJ * 16



def order_mid(tail, head):
    adapters = []
    if tail:
        for t in range(NT + 1):
            if t < NT:
                adapters += [("X2T", t), ("HID", t), ("ADP", t)]
            if t >= 1:
                adapters += [("NORM", t - 1), ("X3T", t - 1), ("LOW", t - 1), ("LORA", t - 1)]
    if not head:
        return adapters
    main = [("IN", n) for n in range(2 * NT)]
    for g in range(NG):
        main += [("Q", g), ("K", g), ("KS", g), ("VS", g)]
    main += [("V", t) for t in range(NT)]
    maxima = [("SMAX", g, u) for g in range(NG) for u in range(2 * NT)]
    opens = {g: 2 * NT + 4 * g + 7 for g in range(NG)}
    out = []
    for i, step in enumerate(main):
        out.append(step)
        if step[0] == "VS":
            out.append(("SELF", step[1]))
        if adapters:
            out.append(adapters.pop(0))
            if i >= 2 * NT and len(adapters) > len(main) - i:
                out.append(adapters.pop(0))
        for _ in range(2):
            if maxima and i >= opens[maxima[0][1]]:
                out.append(maxima.pop(0))
    while maxima or adapters:
        for _ in range(2):
            if maxima:
                out.append(maxima.pop(0))
        if adapters:
            out.append(adapters.pop(0))
    return out + [("MROW",)]


ORDER_L1 = [("PREPB",), ("PREPA",), ("WO", 0), ("WO", 1), ("X1T", 0), ("WO", 2), ("S1", 0), ("X1T", 1),
            ("WO", 3), ("S1", 1), ("P1T", 0), ("X1T", 2), ("PV1", 0), ("S1", 2), ("P1T", 1), ("X1T", 3),
            ("PV1", 1), ("S1", 3), ("P1T", 2), ("PV1", 2), ("P1T", 3), ("PV1", 3)]


def plan_banks():
    uses = {k: [] for k in (0, 1, 2, 3, 4, 6)}

    def give(bank, step):
        uses[bank].append(step)

    n = m = 0
    for step in order_mid(False, True):
        if step[0] in ("IN", "Q", "K", "KS", "VS", "V", "MROW"):
            give(n % 2, step)
            n += 1
        elif step[0] == "SMAX":
            give((4, 6)[m % 2], step)
            m += 1
    for g in range(NG):
        give(3, ("SELF", g))
    for g in range(NG):
        give(2, ("SUM", g))
        give(3, ("PSB", g))
        give(g % 2, ("PV", g))
        for k in range(NT):
            give(4, ("ST", g, k, 0))
            give(6, ("ST", g, k, 1))
    small = {"X1T": (0, 1), "P1T": (1, 0), "S1": (4, 6), "WO": (2, 3), "PV1": (2, 3)}
    for step in ORDER_L1:
        if step[0] in ("PREPA", "PREPB"):
            give(3 if step[0] == "PREPA" else 2, step)
        else:
            give(small[step[0]][step[1] % 2], step)
    for step in order_mid(True, False):
        if step[0] != "NORM":
            give(2, step)
    where = {step: (k, c) for k, steps in uses.items() for c, step in enumerate(steps)}
    return where, {k: len(steps) for k, steps in uses.items()}


WHERE, USES = plan_banks()


def build_program(nc, x, f, len_, stage_, lang_, rlang_, Wq, bq, Wk, bk, Wv, bv, Wo, bo, b_prev, b_self,
                  embed, W1, b1, W2, b2, gamma, beta, lora_A, lora_B, lang_embed, out):
    ctx = ExitStack()
    with ctx:
        def sb(name, shape, dt=F32):
            return ctx.enter_context(nc.sbuf_tensor(name, shape, dt))

        def sem(name):
            return ctx.enter_context(nc.semaphore(name))

        ident = sb("ident", [P, P])
        w_hi = sb("w_hi", [P, 4, ND, D], F16)
        w_lo = sb("w_lo", [P, 4, ND, D], F16)
        vecs = sb("vecs", [20, P])
        cols = sb("cols", [P, 20])
        bias_q = sb("bias_q", [P, NG])
        bias_k = sb("bias_k", [P, NG])
        bias_ks = sb("bias_ks", [P, NG])
        bo_rows = sb("bo_rows", [P, D])
        head_cols = sb("head_cols", [P, NG, H])
        head_rows = sb("head_rows", [H, NG, P])
        ones = sb("ones", [P, DH])
        tiles_in = sb("tiles_in", [P, NT, D])
        xT = sb("xT", [P, 2, ND, S], F16)
        fT = sb("fT", [P, 2, ND, S], F16)
        f_keep = sb("f_keep", [P, NT, D])
        qk32 = sb("qk32", [P, 3, S])
        half = sb("half", [P, 2, 2, 2, S], F16)
        prod = sb("prod", [P, S])
        QS = sb("QS", [P, NJ, NG, S], F16)
        KS = sb("KS", [P, NJ, NG, S], F16)
        V = sb("V", [P, NT, D])
        vsT = sb("vsT", [P, NG, S])
        mx = sb("mx", [P, NT, H])
        self16 = sb("self16", [H, S])
        shift = sb("shift", [H, S], F16)
        big = sb("big", [P, 2, NJ, S])
        t1 = sb("t1", [P, S])
        t2 = sb("t2", [P, S])
        rden = sb("rden", [P, S])
        x1 = sb("x1", [P, NT, D])
        ecol = sb("ecol", [P, 4 + 4 * RANK])
        q1 = sb("q1", [P, 2, D])
        q1T = sb("q1T", [P, 2, 2, ND, P], F16)
        p1 = sb("p1", [P, 2, S])
        p1T = sb("p1T", [P, 2, NT, P])
        nmax = sb("nmax", [P, 2])
        rsum = sb("rsum", [P, 2])
        rrec = sb("rrec", [P, 2])
        hT = sb("hT", [P, 2, P])
        y = sb("y", [P, 2, D])
        st = sb("st", [P, 2, 8])
        lowT = sb("lowT", [RANK + 1, 2, P])
        w1 = sb("w1", [P, ND, A])
        w2 = sb("w2", [P, D])
        b1c = sb("b1c", [P, 1])
        b2r = sb("b2r", [P, D])
        gr = sb("gr", [P, D])
        br = sb("br", [P, D])
        small = sb("small", [RANK, D])
        smallb = sb("smallb", [P, ND, RANK])
        erow = sb("erow", [NT, P])
        lowB = sb("lowB", [RANK + 1, D])
        idx = sb("idx", [1, 4 * B], I32)
        lens_i = sb("lens_i", [B, 1], I32)
        lens_f = sb("lens_f", [B, 1])
        aT = xT
        x2T, xb, x3T, junk = big[:, 0, 0:2], big[:, 0, 2:4], big[:, 1, 0:2], big[:, 1, 2]
        stage32 = [big[:, n].rearrange("p a n -> p (a n)") for n in range(2)]
        stage32 = [s_.rearrange("p (a n) -> p a n", a=ND) for s_ in stage32]
        kpos = t1[0:B, :]
        mask16 = half[0:B, 0, 0, 0, :]
        mask_dram = nc.dram_tensor("mask_rows", (B, S), F16, kind="Internal").ap()

        lone = {k: ctx.enter_context(nc.psum_tensor(f"bank{k}", [P, 512], F32)) for k in range(4)}
        pair = {k: ctx.enter_context(nc.psum_tensor(f"banks{k}", [P, 2, 512], F32)) for k in (4, 6)}
        full = {k: sem(f"full{k}") for k in USES}
        free = {k: sem(f"free{k}") for k in USES}

        def bank(step):
            k = WHERE[step][0]
            return lone[k] if k < 4 else pair[k]

        def wait_free(eng, step, b):
            k, c = WHERE[step]
            eng.wait_ge(free[k], b * USES[k] + c)

        def wait_full(eng, step, b):
            k, c = WHERE[step]
            eng.wait_ge(full[k], b * USES[k] + c + 1)

        def wait_read(eng, step, b):
            k, c = WHERE[step]
            eng.wait_ge(free[k], b * USES[k] + c + 1)

        def done(step):
            return full[WHERE[step][0]]

        def read(step):
            return free[WHERE[step][0]]

        vec_in = sem("vec_in")
        idx_in = sem("idx_in")
        len_in = sem("len_in")
        w_in = [sem("w_in0"), sem("w_in1")]
        consts = sem("consts")
        sel_ready = sem("sel_ready")
        rows_ready = sem("rows_ready")
        w_hi_done = sem("w_hi_done")
        w_lo_done = sem("w_lo_done")
        cols_full = sem("cols_full")
        cols_done = sem("cols_done")
        bias_full = sem("bias_full")
        bias_done = sem("bias_done")
        len_cast = sem("len_cast")
        mask_made = sem("mask_made")
        mask_out = sem("mask_out")
        tile_in = [sem(f"tile_in{n}") for n in range(NT)]
        in_hi = sem("in_hi")
        qk_hi = sem("qk_hi")
        qk_lo = sem("qk_lo")
        stacked = [sem(f"stacked{g}") for g in range(NG)]
        mask_in = sem("mask_in")
        shift_in = sem("shift_in")
        self_diff = sem("self_diff")
        self_exp = sem("self_exp")
        pv_done = sem("pv_done")
        self_part = sem("self_part")
        den_rec = sem("den_rec")
        att_f32 = sem("att_f32")
        att_hi = sem("att_hi")
        att_lo = sem("att_lo")
        x_in = sem("x_in")
        f_in = sem("f_in")
        prep_in = sem("prep_in")
        emb_in = sem("emb_in")
        par_in = sem("par_in")
        x_bo = sem("x_bo")
        q1_done = sem("q1_done")
        q1_hi = sem("q1_hi")
        max1 = sem("max1")
        exp1 = sem("exp1")
        rec1 = sem("rec1")
        xb_done = sem("xb_done")
        xg_done = sem("xg_done")
        mean_done = sem("mean_done")
        sq_done = sem("sq_done")
        newton = sem("newton")
        normed = sem("normed")
        scaled = sem("scaled")
        x3_done = sem("x3_done")
        stored = [sem("stored0"), sem("stored1")]
        NEWTON = 12

        def wait_used(eng, n, i):
            g, k = divmod(n, NT)
            if k == NT - 1:
                wait_full(eng, ("SUM", g), i)
            else:
                eng.wait_ge(pv_done, i * NG * (NT - 1) + g * (NT - 1) + k + 1)

        in_loop = nc.Block()
        block = ctx.enter_context(in_loop)

        def hi_lo(eng, out_ap, left, right, close, fresh=True):
            mm = None
            n = len(left)
            for i, (l, r) in enumerate(zip(left, right)):
                for c, (lh, rh) in enumerate(((0, 0), (1, 0), (0, 1))):
                    mm = eng.matmul(out_ap, l[lh], r[rh], start=(fresh and i == 0 and c == 0),
                                    stop=(close and i == n - 1 and c == 2))
            return mm

        @block.gpsimd
        def _(eng):
            eng.memset(ident[:, :], 0.0).then_inc(consts, 1)
            eng.memset(head_cols[:, :, :], 0.0).then_inc(consts, 1)
            eng.memset(head_rows[:, :, :], 0.0).then_inc(consts, 1)
            eng.memset(ones[:, :], 1.0).then_inc(consts, 1)
            eng.wait_ge(consts, 4)
            eng.affine_select(out=ident[:, :], in_=ident[:, :], compare_op=ALU.not_equal, fill=1.0,
                              base=0, pattern=[[-1, P]], channel_multiplier=1).then_inc(sel_ready, 1)
            for g in range(NG):
                v = head_rows[:, g, :].rearrange("h (j d) -> h j d", j=NJ)
                eng.affine_select(out=v, in_=v, compare_op=ALU.not_equal, fill=1.0, base=-g,
                                  pattern=[[-NG, NJ], [0, DH]], channel_multiplier=1).then_inc(sel_ready, 1)
            eng.iota(kpos, pattern=[[1, S]], base=0, channel_multiplier=0,
                     allow_small_or_imprecise_dtypes=True).then_inc(sel_ready, 1)

            def mid(tail, head, i):
                b = i + 1 if tail else i
                for step in order_mid(tail, head):
                    if step[0] in ("Q", "K"):
                        g, k = step[1], int(step[0] == "K")
                        eng.wait_ge(qk_hi, b * 2 * NG + 2 * g + k + 1)
                        eng.tensor_tensor(half[:, g % 2, k, 1, :], qk32[:, 2 if k else g % 2, :],
                                          half[:, g % 2, k, 0, :], ALU.subtract).then_inc(qk_lo, 1)
                    elif step[0] == "X2T":
                        t = step[1]
                        if t >= 2:
                            wait_read(eng, ("ADP", t - 2), i)
                        else:
                            wait_used(eng, NSTEP - 1, i)
                        if t == 0:
                            eng.wait_ge(par_in, i * 96 + 96)
                        wait_read(eng, ("PV1", t), i)
                        eng.tensor_tensor(xb[:, t % 2, :], x1[:, t, :], b2r[:, :], ALU.add).then_inc(xb_done, 1)
                    elif step[0] == "NORM":
                        t = step[1]
                        wait_full(eng, ("X2T", t), i)
                        eng.wait_ge(xb_done, i * NT + t + 1)
                        eng.tensor_tensor(x1[:, t, :], x1[:, t, :], br[:, :], ALU.add).then_inc(xg_done, 1)
                        eng.wait_ge(normed, i * NT + t + 1)
                        eng.tensor_tensor(y[:, t % 2, :], y[:, t % 2, :], gr[:, :], ALU.mult).then_inc(scaled, 1)
                        eng.wait_ge(scaled, i * NT + t + 1)
                        eng.wait_ge(xg_done, i * NT + t + 1)
                        eng.tensor_tensor(y[:, t % 2, :], y[:, t % 2, :], x1[:, t, :],
                                          ALU.add).then_inc(x3_done, 1)

            def add_bo(i):
                eng.wait_ge(x_in, i * 16 + 16)
                for t in range(NT):
                    eng.tensor_tensor(x1[:, t, :], x1[:, t, :], bo_rows[:, :], ALU.add).then_inc(x_bo, 1)

            eng.wait_ge(vec_in, 6 * 16)
            mid(False, True, 0)
            with eng.Fori(0, B - 1) as i:
                add_bo(i)
                mid(True, True, i)
            add_bo(B - 1)
            mid(True, False, B - 1)

        @block.sync
        def _(eng):
            for n, (v, r) in enumerate(((bq, bq), (bk, bk), (bv, bv), (b_self, b_self), (b_prev, b_prev))):
                flat = v if len(v.shape) == 1 else v.rearrange("a c n -> (a c n)")
                eng.dma_start(vecs[4 * n:4 * n + 4, :], flat.rearrange("(t p) -> t p", p=P)).then_inc(vec_in, 16)
            eng.dma_start(bo_rows[:, :], bo.rearrange("(a n) -> a n", a=1).to_broadcast([P, D])).then_inc(vec_in, 16)
            eng.dma_start(idx[:, 0:B], stage_.rearrange("(a n) -> a n", a=1)).then_inc(idx_in, 16)
            eng.dma_start(idx[:, B:2 * B], lang_.rearrange("(a n) -> a n", a=1)).then_inc(idx_in, 16)
            eng.dma_start(idx[:, 2 * B:3 * B], rlang_.rearrange("(a n) -> a n", a=1)).then_inc(idx_in, 16)
            eng.dma_start(lens_i[:, :], len_.rearrange("(n a) -> n a", a=1)).then_inc(len_in, 16)
            for n, w in enumerate((Wq, Wk, Wv, Wo)):
                if n >= 2:
                    eng.wait_ge(w_lo_done, n - 1)
                    eng.wait_ge(bias_full, 3)
                eng.dma_start(stage32[n % 2], w.rearrange("(t p) n -> p t n", p=P)).then_inc(w_in[n % 2], 16)
            eng.wait_ge(mask_made, 1)
            eng.dma_start(mask_dram, mask16).then_inc(mask_out, 16)
            eng.wait_ge(mask_out, 16)
            eng.wait_ge(idx_in, 48)

            def load_tile(n, b):
                src = x if n < NT else f
                t = n % NT
                if isinstance(b, int):
                    rows = src[b, t * P:(t + 1) * P, :]
                else:
                    rows = src[bass.ds(b, 1), t * P:(t + 1) * P, :].rearrange("a p n -> (a p) n")
                eng.dma_start(tiles_in[:, t, :], rows).then_inc(tile_in[t], 16)

            def whole(src, b):
                if isinstance(b, int):
                    return src[b].rearrange("(t p) n -> p t n", p=P)
                return src[bass.ds(b, 1), :, :].rearrange("a (t p) n -> p (a t) n", p=P)

            def mid(tail, head, i):
                b = i + 1 if tail else i
                for step in order_mid(tail, head):
                    if step[0] == "IN" and step[1] < NT:
                        wait_full(eng, step, b)
                        load_tile(step[1] + NT, b)
                    elif step[0] in ("Q", "K"):
                        g, k = step[1], int(step[0] == "K")
                        if g == 0 and k == 0:
                            row = mask_dram[bass.ds(b, 1), :] if tail else mask_dram[b:b + 1, :]
                            if tail:
                                wait_full(eng, ("ST", NG - 1, NT - 1, 1), i)
                            else:
                                eng.wait_ge(rows_ready, 3 + H)
                            eng.dma_start(KS[MASK_ROW:MASK_ROW + 1, :, :, :].rearrange("o j g n -> o (j g) n"),
                                          row.to_broadcast([H, S]).rearrange("(o h) n -> o h n", o=1)
                                          ).then_inc(mask_in, 16)
                        eng.wait_ge(qk_lo, b * 2 * NG + 2 * g + k + 1)
                        stack = KS if k else QS
                        for r, part in enumerate((0, 1, 0) if k else (0, 0, 1)):
                            for j in range(NJ):
                                eng.dma_start(stack[r * DH:(r + 1) * DH, j, g, :],
                                              half[j * DH:(j + 1) * DH, g % 2, k, part, :]
                                              ).then_inc(stacked[g], 16)
                    elif step[0] == "MROW":
                        wait_read(eng, step, b)
                        eng.dma_start(QS[SHIFT_ROW:SHIFT_ROW + 1, :, :, :].rearrange("o j g n -> o (j g) n"),
                                      shift[:, :]).then_inc(shift_in, 16)
                    elif step[0] == "LORA":
                        t = step[1]
                        wait_read(eng, step, i)
                        if isinstance(i, int):
                            dst = out[i, t * P:(t + 1) * P, :]
                        else:
                            dst = out[bass.ds(i, 1), t * P:(t + 1) * P, :].rearrange("a p n -> (a p) n")
                        eng.dma_start(dst, y[:, t % 2, :]).then_inc(stored[t % 2], 16)

            def params(i):
                stage = eng.value_load(idx[0:1, bass.ds(i, 1)], min_val=0, max_val=STAGES - 1)
                lang = eng.value_load(idx[0:1, bass.ds(i + B, 1)], min_val=0, max_val=LANGS - 1)
                rlang = eng.value_load(idx[0:1, bass.ds(i + 2 * B, 1)], min_val=0, max_val=RLANGS - 1)
                eng.wait_ge(free[2], i * USES[2])
                eng.dma_start(x1[:, :, :], whole(x, i)).then_inc(x_in, 16)
                eng.dma_start(f_keep[:, :, :], whole(f, i)).then_inc(f_in, 16)
                eng.dma_start(erow[:, :], embed[bass.ds(stage, 1), :].rearrange("a (t p) -> (a t) p", p=P)
                              ).then_inc(prep_in, 16)
                eng.dma_start(small[:, :], lora_A[bass.ds(rlang, 1), :, :].rearrange("a r n -> (a r) n")
                              ).then_inc(prep_in, 16)
                eng.dma_start(smallb[:, :, :], lora_B[bass.ds(rlang, 1), :, :].rearrange("a (t p) r -> p (a t) r", p=P)
                              ).then_inc(prep_in, 16)
                eng.dma_start(lowB[RANK:RANK + 1, :], lang_embed[bass.ds(rlang, 1), :]).then_inc(emb_in, 16)
                eng.dma_start(w1[:, :, :], W1[bass.ds(lang, 1), :, :].rearrange("a (t p) n -> p (a t) n", p=P)
                              ).then_inc(par_in, 16)
                eng.dma_start(w2[:, :], W2[bass.ds(lang, 1), :, :].rearrange("a p n -> (a p) n")).then_inc(par_in, 16)
                eng.dma_start(b1c[:, :], b1[bass.ds(lang, 1), :].rearrange("a (p o) -> (a p) o", o=1)
                              ).then_inc(par_in, 16)
                for dst, src in ((b2r, b2), (gr, gamma), (br, beta)):
                    eng.dma_start(dst[:, :], src[bass.ds(lang, 1), :].to_broadcast([P, D])).then_inc(par_in, 16)

            def prefetch(i):
                for t in range(NT):
                    wait_full(eng, ("IN", NT + t), i)
                    load_tile(t, i + 1)

            for t in range(NT):
                load_tile(t, 0)
            mid(False, True, 0)
            with eng.Fori(0, B - 1) as i:
                params(i)
                prefetch(i)
                mid(True, True, i)
            params(B - 1)
            mid(True, False, B - 1)
            for n in range(2):
                eng.wait_ge(stored[n], B * NT // 2 * 16)

        @block.scalar
        def _(eng):
            for n in range(4):
                eng.wait_ge(w_in[n % 2], 16 * (n // 2 + 1))
                eng.activation(w_hi[:, n, :, :], stage32[n % 2], ACT.Copy, scale=WS).then_inc(w_hi_done, 1)
            eng.wait_ge(bias_done, 3)

            def mid(tail, head, i):
                b = i + 1 if tail else i
                for step in order_mid(tail, head):
                    kind = step[0]
                    if kind == "IN":
                        n = step[1]
                        dst = (xT if n < NT else fT)[:, 0, :, (n % NT) * P:(n % NT + 1) * P]
                        wait_full(eng, step, b)
                        eng.activation(dst, bank(step)[:, :].rearrange("p (t n) -> p t n", t=ND), ACT.Copy
                                       ).then_inc(in_hi, 1)
                    elif kind in ("Q", "K"):
                        g, k = step[1], int(kind == "K")
                        wait_full(eng, step, b)
                        if k:
                            eng.wait_ge(qk_lo, b * 2 * NG + 2 * g)
                        elif g >= 2:
                            eng.wait_ge(qk_lo, b * 2 * NG + 2 * g - 3)
                            wait_read(eng, ("KS", g - 2), b)
                        elif tail:
                            eng.wait_ge(qk_lo, i * 2 * NG + 2 * NG - 3 + 2 * g)
                            wait_read(eng, ("KS", NG - 2 + g), i)
                        eng.activation(qk32[:, 2 if k else g % 2, :], bank(step)[:, :], ACT.Identity,
                                       bias=(bias_k if k else bias_q)[:, g:g + 1], scale=1.0 / WS
                                       ).then_inc(read(step), 1)
                    elif kind == "VS":
                        wait_full(eng, step, b)
                        eng.activation(vsT[:, step[1], :], bank(step)[:, :], ACT.Copy, scale=1.0 / WS
                                       ).then_inc(read(step), 1)
                    elif kind == "V":
                        wait_full(eng, step, b)
                        eng.activation(V[:, step[1], :], bank(step)[:, :], ACT.Copy, scale=1.0 / WS
                                       ).then_inc(read(step), 1)
                    elif kind == "MROW":
                        wait_full(eng, ("SELF", NG - 1), b)
                        eng.activation(self16[:, :], lone[3][0:H, :], ACT.Copy, scale=-1.0
                                       ).then_inc(read(("SELF", 0)), NG)
                        eng.wait_ge(self_diff, b + 1)
                        eng.activation(self16[:, :], self16[:, :], ACT.Exp, scale=SCALE).then_inc(self_exp, 1)
                    elif kind == "X2T":
                        t = step[1]
                        wait_full(eng, step, i)
                        eng.activation(x2T[:, t % 2, :], lone[2][:, :], ACT.Copy).then_inc(read(step), 1)
                    elif kind == "HID":
                        t = step[1]
                        if t == 0:
                            eng.wait_ge(par_in, i * 96 + 96)
                        wait_full(eng, step, i)
                        eng.activation(hT[:, t % 2, :], lone[2][:, 0:P], ACT.Relu, bias=b1c[:, :]
                                       ).then_inc(read(step), 1)
                    elif kind == "ADP":
                        t = step[1]
                        eng.wait_ge(mean_done, i * NT + t + 1)
                        eng.activation(junk, y[:, t % 2, :], ACT.Square, bias=st[:, t % 2, 1:2],
                                       accum_out=st[:, t % 2, 2:3]).then_inc(sq_done, 1)
                    elif kind == "X3T":
                        t = step[1]
                        wait_full(eng, step, i)
                        eng.activation(x3T[:, t % 2, :], lone[2][:, :], ACT.Copy).then_inc(read(step), 1)
                    elif kind == "LOW":
                        t = step[1]
                        wait_full(eng, step, i)
                        eng.activation(lowT[0:RANK, t % 2, :], lone[2][0:RANK, 0:P], ACT.Copy
                                       ).then_inc(read(step), 1)

            def att_half(g, i):
                eng.wait_ge(att_f32, i * NG + g + 1)
                eng.activation(aT[:, 0, g, :], t2[:, :], ACT.Identity, bias=cols[:, 8 + g:9 + g]
                               ).then_inc(att_hi, 1)

            def attention(i):
                eng.wait_ge(free[2], i * USES[2])
                for n in range(NSTEP):
                    g, k = divmod(n, NT)
                    if n >= 2:
                        wait_used(eng, n - 2, i)
                    for u in range(2):
                        step = ("ST", g, k, u)
                        wait_full(eng, step, i)
                        eng.activation(big[:, n % 2, 2 * u:2 * u + 2, :], bank(step)[:, :, :], ACT.Exp, scale=SCALE
                                       ).then_inc(read(step), 1)
                    if k == 1 and g >= 1:
                        att_half(g - 1, i)
                att_half(NG - 1, i)

            def layer1(i):
                for step in ORDER_L1:
                    kind = step[0]
                    t = step[-1]
                    if kind == "PREPA":
                        wait_full(eng, step, i)
                        eng.activation(ecol[:, :], lone[3][:, 0:4 + 4 * RANK], ACT.Copy).then_inc(read(step), 1)
                    elif kind == "PREPB":
                        wait_full(eng, step, i)
                        eng.activation(lowB[0:RANK, :], lone[2][0:RANK, :], ACT.Copy).then_inc(read(step), 1)
                    elif kind == "X1T":
                        wait_full(eng, step, i)
                        eng.activation(q1T[:, t % 2, 0, :, :], bank(step)[:, :].rearrange("p (t n) -> p t n", t=ND),
                                       ACT.Copy).then_inc(q1_hi, 1)
                    elif kind == "WO":
                        wait_read(eng, ("PREPA",), i)
                        wait_read(eng, step, i)
                        if t >= 2:
                            wait_full(eng, ("X1T", t - 2), i)
                        eng.activation(q1[:, t % 2, :], x1[:, t, :], ACT.Identity, bias=ecol[:, t:t + 1]
                                       ).then_inc(q1_done, 1)
                    elif kind == "S1":
                        eng.wait_ge(max1, i * NT + t + 1)
                        if t >= 2:
                            wait_full(eng, ("P1T", t - 2), i)
                        eng.activation(p1[:, t % 2, :], bank(step)[:, 0, :], ACT.Exp, bias=nmax[:, t % 2:t % 2 + 1],
                                       accum_out=rsum[:, t % 2:t % 2 + 1]).then_inc(read(step), 1)
                    elif kind == "P1T":
                        wait_full(eng, step, i)
                        if t >= 2:
                            wait_full(eng, ("PV1", t - 2), i)
                        eng.activation(p1T[:, t % 2, :, :], bank(step)[:, :].rearrange("p (t n) -> p t n", t=NT),
                                       ACT.Copy).then_inc(read(step), 1)

            mid(False, True, 0)
            with eng.Fori(0, B - 1) as i:
                attention(i)
                layer1(i)
                mid(True, True, i)
            attention(B - 1)
            layer1(B - 1)
            mid(True, False, B - 1)

        @block.vector
        def _(eng):
            eng.memset(QS[MASK_ROW:P, :, :, :], BIG).then_inc(rows_ready, 1)
            eng.memset(KS[MASK_ROW:P, :, :, :], 1.0).then_inc(rows_ready, 1)
            eng.memset(lowT[:, :, :], 1.0).then_inc(rows_ready, 1)
            eng.wait_ge(consts, 4)
            for j in range(NJ):
                for g in range(NG):
                    eng.memset(head_cols[DH * j:DH * j + DH, g, NG * j + g:NG * j + g + 1], 1.0 / WS
                               ).then_inc(rows_ready, 1)
            eng.wait_ge(len_in, 16)
            eng.tensor_copy(lens_f[:, :], lens_i[:, :]).then_inc(len_cast, 1)
            eng.wait_ge(len_cast, 1)
            eng.wait_ge(sel_ready, 1 + NG + 1)
            eng.tensor_scalar(mask16, kpos, lens_f[:, 0:1], -BIG, ALU.is_ge, ALU.mult).then_inc(mask_made, 1)
            for n in range(4):
                eng.wait_ge(w_hi_done, n + 1)
                eng.scalar_tensor_tensor(out=w_lo[:, n, :, :], in0=stage32[n % 2], scalar=WS, in1=w_hi[:, n, :, :],
                                         op0=ALU.mult, op1=ALU.subtract).then_inc(w_lo_done, 1)
                if n == 1:
                    eng.wait_ge(cols_full, 1)
                    eng.tensor_copy(cols[:, :], lone[0][:, 0:20]).then_inc(cols_done, 1)
                    eng.wait_ge(cols_done, 1)
                    eng.wait_ge(bias_full, 3)
                    eng.tensor_tensor(bias_q[:, :], lone[1][:, 0:4], cols[:, 0:4], ALU.add).then_inc(bias_done, 1)
                    eng.tensor_tensor(bias_k[:, :], lone[1][:, 4:8], cols[:, 4:8], ALU.add).then_inc(bias_done, 1)
                    eng.tensor_tensor(t2[:, 0:4], lone[1][:, 8:12], cols[:, 4:8], ALU.add).then_inc(cols_done, 1)
                    eng.wait_ge(cols_done, 2)
                    eng.tensor_scalar(bias_ks[:, :], t2[:, 0:4], WS, None, ALU.mult).then_inc(bias_done, 1)
            eng.wait_ge(bias_done, 3)
            eng.wait_ge(mask_out, 16)

            def mid(tail, head, i):
                b = i + 1 if tail else i
                for step in order_mid(tail, head):
                    kind = step[0]
                    if kind == "IN":
                        n = step[1]
                        big_t = xT if n < NT else fT
                        at = slice((n % NT) * P, (n % NT + 1) * P)
                        eng.wait_ge(in_hi, b * 2 * NT + n + 1)
                        eng.tensor_tensor(big_t[:, 1, :, at], bank(step)[:, :].rearrange("p (t n) -> p t n", t=ND),
                                          big_t[:, 0, :, at], ALU.subtract).then_inc(read(step), 1)
                    elif kind in ("Q", "K"):
                        g, k = step[1], int(kind == "K")
                        wait_read(eng, step, b)
                        if g >= 2:
                            eng.wait_ge(stacked[g - 2], b * DMAS_PER_STACK + DMAS_PER_STACK)
                        elif tail:
                            eng.wait_ge(stacked[NG - 2 + g], i * DMAS_PER_STACK + DMAS_PER_STACK)
                        eng.tensor_copy(half[:, g % 2, k, 0, :], qk32[:, 2 if k else g % 2, :]).then_inc(qk_hi, 1)
                    elif kind == "KS":
                        g = step[1]
                        wait_full(eng, step, b)
                        if g >= 1:
                            wait_full(eng, ("SELF", g - 1), b)
                        elif tail:
                            wait_full(eng, ("SELF", NG - 1), i)
                        eng.scalar_tensor_tensor(out=prod[:, :], in0=bank(step)[:, :], scalar=bias_ks[:, g:g + 1],
                                                 in1=qk32[:, g % 2, :], op0=ALU.add, op1=ALU.mult
                                                 ).then_inc(read(step), 1)
                    elif kind == "SMAX":
                        _, g, u = step
                        t, q = divmod(u, 2)
                        wait_full(eng, step, b)
                        eng.tensor_reduce(mx[:, t, 2 * q * NG + g:2 * q * NG + g + NG + 1:NG],
                                          bank(step)[:, :, :], AX_X, ALU.max).then_inc(read(step), 1)
                    elif kind == "MROW":
                        wait_full(eng, step, b)
                        wait_read(eng, ("SELF", NG - 1), b)
                        if tail:
                            eng.wait_ge(shift_in, b * 16)
                        eng.scalar_tensor_tensor(out=shift[:, :], in0=bank(step)[0:H, :], scalar=-1.0,
                                                 in1=self16[:, :], op0=ALU.mult, op1=ALU.min
                                                 ).then_inc(read(step), 1)
                        wait_read(eng, step, b)
                        eng.tensor_tensor(self16[:, :], shift[:, :], self16[:, :], ALU.subtract
                                          ).then_inc(self_diff, 1)
                    elif kind == "ADP":
                        t = step[1]
                        wait_full(eng, step, i)
                        eng.wait_ge(xb_done, i * NT + t + 1)
                        if t >= 2:
                            eng.wait_ge(stored[t % 2], i * NT // 2 * 16 + (t // 2) * 16)
                        elif tail:
                            eng.wait_ge(stored[t % 2], i * (NT // 2 * 16))
                        eng.scalar_tensor_tensor(out=y[:, t % 2, :], in0=lone[2][:, :], scalar=1.0,
                                                 in1=xb[:, t % 2, :], op0=ALU.mult, op1=ALU.add,
                                                 accum_out=st[:, t % 2, 0:1]).then_inc(read(step), 1)
                        wait_read(eng, step, i)
                        eng.tensor_scalar(st[:, t % 2, 1:2], st[:, t % 2, 0:1], -1.0 / D, None, ALU.mult
                                          ).then_inc(mean_done, 1)
                    elif kind == "NORM":
                        t = step[1]
                        s_ = st[:, t % 2, :]
                        si = s_.bitcast(I32)
                        var, r, c = s_[:, 3:4], s_[:, 4:5], s_[:, 5:6]
                        base = i * (NT * NEWTON) + t * NEWTON
                        eng.wait_ge(sq_done, i * NT + t + 1)
                        eng.tensor_scalar(var, s_[:, 2:3], 1.0 / D, EPS, ALU.mult, ALU.add).then_inc(newton, 1)
                        eng.wait_ge(newton, base + 1)
                        eng.tensor_scalar(si[:, 5:6], si[:, 3:4], 1, None, ALU.logical_shift_right).then_inc(newton, 1)
                        eng.wait_ge(newton, base + 2)
                        eng.tensor_scalar(si[:, 4:5], si[:, 5:6], -1, 0x5F3759DF, ALU.mult, ALU.add).then_inc(newton, 1)
                        for n in range(3):
                            eng.wait_ge(newton, base + 3 + 3 * n)
                            eng.scalar_tensor_tensor(out=c, in0=r, scalar=r, in1=var, op0=ALU.mult,
                                                     op1=ALU.mult).then_inc(newton, 1)
                            eng.wait_ge(newton, base + 4 + 3 * n)
                            eng.tensor_scalar(c, c, -0.5, 1.5, ALU.mult, ALU.add).then_inc(newton, 1)
                            eng.wait_ge(newton, base + 5 + 3 * n)
                            eng.tensor_tensor(r, r, c, ALU.mult).then_inc(newton, 1)
                        eng.wait_ge(newton, base + NEWTON)
                        eng.tensor_scalar(y[:, t % 2, :], y[:, t % 2, :], s_[:, 1:2], r, ALU.add, ALU.mult
                                          ).then_inc(normed, 1)
                    elif kind == "LORA":
                        t = step[1]
                        wait_full(eng, step, i)
                        eng.tensor_tensor(y[:, t % 2, :], lone[2][:, :], y[:, t % 2, :], ALU.add
                                          ).then_inc(read(step), 1)

            def finish_group(g, i):
                wait_full(eng, ("PSB", g), i)
                wait_read(eng, ("VS", g), i)
                eng.tensor_tensor(t1[:, :], lone[3][:, :], vsT[:, g, :], ALU.mult).then_inc(read(("PSB", g)), 1)
                wait_full(eng, ("SUM", g), i)
                eng.reciprocal(rden[:, :], lone[2][:, :]).then_inc(read(("SUM", g)), 1)
                wait_read(eng, ("PSB", g), i)
                if g:
                    eng.wait_ge(att_lo, i * NG + g)
                wait_full(eng, ("PV", g), i)
                eng.tensor_tensor(t1[:, :], bank(("PV", g))[:, :], t1[:, :], ALU.add).then_inc(read(("PV", g)), 1)
                wait_read(eng, ("PV", g), i)
                wait_read(eng, ("SUM", g), i)
                eng.tensor_tensor(t2[:, :], t1[:, :], rden[:, :], ALU.mult).then_inc(att_f32, 1)
                eng.wait_ge(att_hi, i * NG + g + 1)
                eng.scalar_tensor_tensor(out=aT[:, 1, g, :], in0=t2[:, :], scalar=cols[:, 8 + g:9 + g],
                                         in1=aT[:, 0, g, :], op0=ALU.add, op1=ALU.subtract).then_inc(att_lo, 1)

            def attention(i):
                for g in range(NG):
                    finish_group(g, i)

            def layer1(i):
                for step in ORDER_L1:
                    kind, t = step[0], step[-1]
                    if kind == "WO":
                        eng.wait_ge(x_bo, i * NT + t + 1)
                        wait_full(eng, step, i)
                        eng.scalar_tensor_tensor(out=x1[:, t, :], in0=bank(step)[:, :], scalar=1.0 / WS,
                                                 in1=x1[:, t, :], op0=ALU.mult, op1=ALU.add
                                                 ).then_inc(read(step), 1)
                    elif kind == "X1T":
                        eng.wait_ge(q1_hi, i * NT + t + 1)
                        eng.tensor_tensor(q1T[:, t % 2, 1, :, :], bank(step)[:, :].rearrange("p (t n) -> p t n", t=ND),
                                          q1T[:, t % 2, 0, :, :], ALU.subtract).then_inc(read(step), 1)
                    elif kind == "S1":
                        wait_full(eng, step, i)
                        if t >= 2:
                            wait_read(eng, ("S1", t - 2), i)
                        eng.tensor_reduce(nmax[:, t % 2:t % 2 + 1], bank(step)[:, 0, :], AX_X, ALU.max,
                                          negate=True).then_inc(max1, 1)
                    elif kind == "P1T":
                        wait_read(eng, ("S1", t), i)
                        eng.reciprocal(rrec[:, t % 2:t % 2 + 1], rsum[:, t % 2:t % 2 + 1]).then_inc(rec1, 1)
                    elif kind == "PV1":
                        eng.wait_ge(rec1, i * NT + t + 1)
                        wait_full(eng, step, i)
                        eng.wait_ge(q1_done, i * NT + t + 1)
                        eng.scalar_tensor_tensor(out=x1[:, t, :], in0=bank(step)[:, :],
                                                 scalar=rrec[:, t % 2:t % 2 + 1], in1=x1[:, t, :],
                                                 op0=ALU.mult, op1=ALU.add).then_inc(read(step), 1)

            mid(False, True, 0)
            with eng.Fori(0, B - 1) as i:
                attention(i)
                layer1(i)
                mid(True, True, i)
            attention(B - 1)
            layer1(B - 1)
            mid(True, False, B - 1)

        @block.tensor
        def _(eng):
            eng.wait_ge(sel_ready, 1 + NG + 1)
            eng.wait_ge(vec_in, 96)
            eng.transpose(lone[0][:, 0:20], vecs[:, :], ident[0:20, 0:20]).then_inc(cols_full, 1)
            eng.wait_ge(cols_done, 1)
            for n, (w, v) in enumerate(((0, 12), (1, 16), (1, 12))):
                eng.wait_ge(w_in[w], 16)
                mm = None
                for g in range(NG):
                    for d in range(ND):
                        mm = eng.matmul(lone[1][:, 4 * n + g:4 * n + g + 1], stage32[w][:, d, g * P:(g + 1) * P],
                                        cols[:, v + d:v + d + 1], start=(d == 0), stop=(d == ND - 1))
                mm.then_inc(bias_full, 1)
            eng.wait_ge(bias_done, 3)
            eng.wait_ge(w_lo_done, 4)
            eng.wait_ge(rows_ready, 3 + H)

            def weights(w, d, n):
                at = slice(n * P, (n + 1) * P)
                return w_hi[:, w, d, at], w_lo[:, w, d, at]

            def transpose4(step, src, signal):
                for d in range(4):
                    mm = eng.transpose(bank(step)[:, d * P:(d + 1) * P], src[:, d * P:(d + 1) * P], ident[:, :])
                mm.then_inc(signal, 1)

            def mid(tail, head, i):
                b = i + 1 if tail else i
                for step in order_mid(tail, head):
                    kind = step[0]
                    if kind == "IN":
                        n = step[1]
                        eng.wait_ge(tile_in[n % NT], b * 32 + (16 if n < NT else 32))
                        wait_free(eng, step, b)
                        transpose4(step, tiles_in[:, n % NT, :], done(step))
                    elif kind in ("Q", "K", "KS", "VS"):
                        g = step[1]
                        w = {"Q": 0, "K": 1, "KS": 1, "VS": 2}[kind]
                        src = xT if kind == "K" else fT
                        if kind == "Q" and g == 0:
                            wait_read(eng, ("IN", 2 * NT - 2), b)
                            wait_read(eng, ("IN", 2 * NT - 1), b)
                        wait_free(eng, step, b)
                        hi_lo(eng, bank(step)[:, :], [weights(w, d, g) for d in range(ND)],
                              [(src[:, 0, d, :], src[:, 1, d, :]) for d in range(ND)], True
                              ).then_inc(done(step), 1)
                    elif kind == "V":
                        t = step[1]
                        at = slice(t * P, (t + 1) * P)
                        wait_free(eng, step, b)
                        hi_lo(eng, bank(step)[:, :], [(xT[:, 0, d, at], xT[:, 1, d, at]) for d in range(ND)],
                              [(w_hi[:, 2, d, :], w_lo[:, 2, d, :]) for d in range(ND)], True
                              ).then_inc(done(step), 1)
                    elif kind == "SELF":
                        g = step[1]
                        if g == 0:
                            wait_free(eng, step, b)
                        wait_read(eng, ("KS", g), b)
                        eng.matmul(lone[3][0:H, :], head_cols[:, g, :], prod[:, :], start=(g == 0),
                                   stop=(g == NG - 1), skip_group_check=True).then_inc(done(step), 1)
                    elif kind == "SMAX":
                        _, g, u = step
                        t, q = divmod(u, 2)
                        if u == 0:
                            eng.wait_ge(stacked[g], b * DMAS_PER_STACK + DMAS_PER_STACK)
                            if g == 0:
                                eng.wait_ge(mask_in, b * 16 + 16)
                        wait_free(eng, step, b)
                        for j in (2 * q, 2 * q + 1):
                            mm = eng.matmul(bank(step)[:, j % 2, :], QS[0:SHIFT_ROW, j, g, t * P:(t + 1) * P],
                                            KS[0:SHIFT_ROW, j, g, :], start=True, stop=True)
                        mm.then_inc(done(step), 1)
                    elif kind == "MROW":
                        wait_read(eng, ("SMAX", NG - 1, 2 * NT - 2), b)
                        wait_read(eng, ("SMAX", NG - 1, 2 * NT - 1), b)
                        wait_free(eng, step, b)
                        for t in range(NT):
                            mm = eng.transpose(bank(step)[0:H, t * P:(t + 1) * P], mx[:, t, :], ident[:, :])
                        mm.then_inc(done(step), 1)
                    elif kind == "X2T":
                        t = step[1]
                        wait_read(eng, ("PV1", t), i)
                        wait_free(eng, step, i)
                        transpose4(step, x1[:, t, :], done(step))
                    elif kind == "HID":
                        t = step[1]
                        if t == 0:
                            eng.wait_ge(par_in, i * 96 + 96)
                        wait_free(eng, step, i)
                        for d in range(ND):
                            mm = eng.matmul(lone[2][:, 0:P], w1[:, d, :], x2T[:, t % 2, d * P:(d + 1) * P],
                                            start=(d == 0), stop=(d == ND - 1))
                        mm.then_inc(done(step), 1)
                    elif kind == "ADP":
                        wait_free(eng, step, i)
                        eng.matmul(lone[2][:, :], hT[:, step[1] % 2, :], w2[:, :], start=True, stop=True
                                   ).then_inc(done(step), 1)
                    elif kind == "X3T":
                        t = step[1]
                        eng.wait_ge(x3_done, i * NT + t + 1)
                        wait_free(eng, step, i)
                        transpose4(step, y[:, t % 2, :], done(step))
                    elif kind == "LOW":
                        t = step[1]
                        wait_free(eng, step, i)
                        for d in range(ND):
                            mm = eng.matmul(lone[2][0:RANK, 0:P], ecol[:, 4 + d * RANK:4 + (d + 1) * RANK],
                                            x3T[:, t % 2, d * P:(d + 1) * P], start=(d == 0), stop=(d == ND - 1))
                        mm.then_inc(done(step), 1)
                    elif kind == "LORA":
                        if step[1] == 0:
                            eng.wait_ge(emb_in, i * 16 + 16)
                        wait_free(eng, step, i)
                        eng.matmul(lone[2][:, :], lowT[:, step[1] % 2, :], lowB[:, :], start=True, stop=True
                                   ).then_inc(done(step), 1)

            def scores(n, i):
                g, k = divmod(n, NT)
                for u in range(2):
                    step = ("ST", g, k, u)
                    wait_free(eng, step, i)
                    for j in (2 * u, 2 * u + 1):
                        mm = eng.matmul(bank(step)[:, j % 2, :], KS[0:SHIFT_ROW + 1, j, g, k * P:(k + 1) * P],
                                        QS[0:SHIFT_ROW + 1, j, g, :], start=True, stop=True)
                    mm.then_inc(done(step), 1)

            def values(n, i):
                g, k = divmod(n, NT)
                if k == 0:
                    wait_free(eng, ("PSB", g), i)
                    eng.matmul(lone[3][:, :], head_rows[:, g, :], self16[:, :], start=True, stop=True
                               ).then_inc(done(("PSB", g)), 1)
                    wait_free(eng, ("SUM", g), i)
                    eng.matmul(lone[2][:, :], head_rows[:, g, :], self16[:, :], start=True, stop=False,
                               skip_group_check=True)
                    wait_free(eng, ("PV", g), i)
                for u in range(2):
                    wait_read(eng, ("ST", g, k, u), i)
                for j in range(NJ):
                    q = slice(j * DH, (j + 1) * DH)
                    mm = eng.matmul(bank(("PV", g))[q, :], V[:, k, g * P + j * DH:g * P + (j + 1) * DH],
                                    big[:, n % 2, j, :], start=(k == 0), stop=(k == NT - 1), skip_group_check=True)
                if k == NT - 1:
                    mm.then_inc(done(("PV", g)), 1)
                for j in range(NJ):
                    q = slice(j * DH, (j + 1) * DH)
                    mm = eng.matmul(lone[2][q, :], ones[:, :], big[:, n % 2, j, :], start=False,
                                    stop=(k == NT - 1), skip_group_check=True)
                mm.then_inc(pv_done if k < NT - 1 else done(("SUM", g)), 1)

            def attention(i):
                eng.wait_ge(shift_in, i * 16 + 16)
                eng.wait_ge(self_exp, i + 1)
                for t in range(NT):
                    wait_read(eng, ("V", t), i)
                scores(0, i)
                for n in range(NSTEP):
                    if n + 1 < NSTEP:
                        scores(n + 1, i)
                    values(n, i)

            def layer1(i):
                for step in ORDER_L1:
                    kind, t = step[0], step[-1]
                    if kind == "PREPB":
                        eng.wait_ge(prep_in, i * 48 + 48)
                        wait_free(eng, ("PREPA",), i)
                        wait_free(eng, step, i)
                        for d in range(ND):
                            mm = eng.transpose(lone[2][0:RANK, d * P:(d + 1) * P], smallb[:, d, :], ident[:, :])
                        mm.then_inc(done(step), 1)
                    elif kind == "PREPA":
                        eng.transpose(lone[3][:, 0:4], erow[:, :], ident[0:NT, 0:NT])
                        for d in range(ND):
                            mm = eng.transpose(lone[3][:, 4 + d * RANK:4 + (d + 1) * RANK],
                                               small[:, d * P:(d + 1) * P], ident[0:RANK, 0:RANK])
                        mm.then_inc(done(step), 1)
                    elif kind == "WO":
                        if t == 0:
                            eng.wait_ge(att_lo, i * NG + NG)
                        at = slice(t * P, (t + 1) * P)
                        wait_free(eng, step, i)
                        hi_lo(eng, bank(step)[:, :], [(aT[:, 0, g, at], aT[:, 1, g, at]) for g in range(NG)],
                              [(w_hi[:, 3, g, :], w_lo[:, 3, g, :]) for g in range(NG)], True
                              ).then_inc(done(step), 1)
                    elif kind == "X1T":
                        eng.wait_ge(q1_done, i * NT + t + 1)
                        wait_free(eng, step, i)
                        transpose4(step, q1[:, t % 2, :], done(step))
                    elif kind == "S1":
                        wait_read(eng, ("X1T", t), i)
                        wait_free(eng, step, i)
                        hi_lo(eng, bank(step)[:, 0, :],
                              [(q1T[:, t % 2, 0, d, :], q1T[:, t % 2, 1, d, :]) for d in range(ND)],
                              [(fT[:, 0, d, :], fT[:, 1, d, :]) for d in range(ND)], True).then_inc(done(step), 1)
                    elif kind == "P1T":
                        wait_read(eng, ("S1", t), i)
                        wait_free(eng, step, i)
                        transpose4(step, p1[:, t % 2, :], done(step))
                    elif kind == "PV1":
                        if t == 0:
                            eng.wait_ge(f_in, i * 16 + 16)
                        wait_read(eng, ("P1T", t), i)
                        wait_free(eng, step, i)
                        for k in range(NT):
                            mm = eng.matmul(bank(step)[:, :], p1T[:, t % 2, k, :], f_keep[:, k, :],
                                            start=(k == 0), stop=(k == NT - 1))
                        mm.then_inc(done(step), 1)

            mid(False, True, 0)
            with eng.Fori(0, B - 1) as i:
                attention(i)
                layer1(i)
                mid(True, True, i)
            attention(B - 1)
            layer1(B - 1)
            mid(True, False, B - 1)


_INS = ['x', 'fside_BxSxS_0', 'itok_B_18_1004', 'itok_B_0_5', 'itok_B_0_8', 'itok_B_0_3',
        'L0_cond_Wq', 'L0_cond_bq', 'L0_cond_Wk', 'L0_cond_bk', 'L0_cond_Wv', 'L0_cond_bv', 'L0_cond_Wo',
        'L0_cond_bo', 'L0_cond_b_prev', 'L0_cond_b_self', 'L1_cond_braak_embed', 'L2_cond_W1', 'L2_cond_b1',
        'L2_cond_W2', 'L2_cond_b2', 'L2_cond_gamma', 'L2_cond_beta', 'L3_cond_lora_A', 'L3_cond_lora_B',
        'L3_cond_lang_embed']
_OUTS = [((B, S, D), 'float32')]


def kernel(**inputs):
    import numpy as _np
    import concourse.bacc as _bacc
    from concourse import mybir as _mybir
    from concourse.bass_utils import run_bass_kernel_spmd as _run

    nc = _bacc.Bacc("TRN2", target_bir_lowering=False, num_devices=1)
    arrays, args = {}, []
    for name in _INS:
        a = _np.ascontiguousarray(inputs[name])
        arrays[f"in_{name}_dram"] = a
        args.append(nc.dram_tensor(f"in_{name}_dram", a.shape, _mybir.dt.from_np(a.dtype), kind="ExternalInput").ap())
    for n, (shape, dtype) in enumerate(_OUTS):
        dt = _mybir.dt.from_np(_np.dtype(dtype))
        args.append(nc.dram_tensor(f"out_{n}_dram", shape, dt, kind="ExternalOutput").ap())
    build_program(nc, *args)
    r = _run(nc, [arrays], core_ids=[0])
    got = tuple(r.results[0][f"out_{n}_dram"] for n in range(len(_OUTS)))
    return got[0]
```

```python
from contextlib import ExitStack

import concourse.bass as bass
from concourse import mybir

F32 = mybir.dt.float32
F16 = mybir.dt.float16
I32 = mybir.dt.int32
ALU = mybir.AluOpType
ACT = mybir.ActivationFunctionType
AX_X = mybir.AxisListType.X

B, S, D = 8, 512, 512
H, DH = 16, 32
P = 128
NT = S // P
ND = D // P
NG, NJ = H // 4, 4
NSTEP = NG * NT
STAGES, LANGS, A, RLANGS, RANK = 6, 10, 128, 4, 16
SCALE = 1.0 / float(DH) ** 0.5
EPS = 1e-5
WS = 64.0
BIG = 32768.0
RS = 1024.0
PS = 1024.0
MASK_ROW = 3 * DH
SHIFT_ROW = MASK_ROW + 1
DMAS_PER_STACK = 3 * NJ * 16
LOW_ROW = 32
NROWS = LOW_ROW + H



def order_mid(tail, head):
    adapters = []
    if tail:
        n0, n2 = ([("NORM", t, n) for n in range(NORM_PIECES)] for t in (0, 2))
        adapters = [("X2T", 0), None, ("HID", 0), None, ("ADP", 0), None, ("X2T", 1), ("SQ", 0), ("HID", 1), None, ("ADP", 1), None,
                    ("SQ", 1), n0[0], ("X2T", 2), n0[1], ("HID", 2), n0[2], ("X2T", 3), n0[3], ("HID", 3), n0[4],
                    n0[5], None, ("SCALE", 0), None, ("SCALE", 1), ("X3T", 0), None, ("LOW", 0), None, ("ADP", 2),
                    None, ("ADP", 3), ("SQ", 2), ("LORA", 0), ("SQ", 3), ("X3T", 1), n2[0], ("LOW", 1), n2[1],
                    n2[2], ("LORA", 1), n2[3], n2[4], n2[5], None, ("SCALE", 2), None, ("SCALE", 3), None,
                    ("X3T", 2), None, ("LOW", 2), None, ("LORA", 2), None, ("X3T", 3), None, ("LOW", 3), None,
                    ("LORA", 3)]
    if not head:
        return [step for step in adapters if step]


    def parts(step):
        return [("PART", n, step) for n in range(PARTS - 1)] + [step]

    slots = [("IN", NT), ("IN", NT + 1), ("PART", 0, ("K", 0)), ("IN", NT + 2), ("PART", 1, ("K", 0)),
             ("IN", NT + 3), ("K", 0)] + parts(("Q", 0)) + parts(("KS", 0))
    for g in range(1, NG):
        slots += parts(("K", g)) + parts(("Q", g)) + parts(("KS", g))
    for kind in ("VS", "V"):
        for n in range(NG):
            slots += parts((kind, n))
    opens = [slots.index(("Q", g)) + OPEN[g] for g in range(NG)]
    maxima = [("SMAX", g, u) for g in range(NG) for u in range(2 * NT)]
    out, later = [], {}
    rows = sums = False
    for i, step in enumerate(slots):
        out.append(step)
        out += later.get(i, [])
        if maxima and i >= opens[maxima[0][1]]:
            out.append(maxima.pop(0))
        elif not maxima and not rows:
            out.append(("MROW",))
            rows = True
            late = i + PARTS
        if adapters:
            out += [a for a in (adapters.pop(0),) if a]
        if rows and not sums and i >= late and not adapters:
            out.append(("SROW",))
            sums = True
        if step[0] in ("K", "Q"):
            later[i + 1] = [("HALF",) + step]
        if step[0] == "KS":
            later[i + 2 * PARTS] = [("SELF", step[1])]
        if step == ("VS", 2):
            later[i + PARTS - 1] = [("NEG",)]
    assert rows and i >= max(later)
    return out + [a for a in adapters if a] + ([] if sums else [("SROW",)])


OPEN = (16, 13, 13, 15)
PARTS = 3
NEWTON = 15
NORM_PIECES = 6

ORDER_L1 = [("WOP", 0), ("WOP", 1), ("WO", 0), ("WOP", 2), ("WO", 1), ("X1T", 0), ("WOP", 3), ("X1T", 1),
            ("WO", 2), ("WO", 3), ("S1", 0), ("X1T", 2), ("S1", 1), ("X1T", 3), ("P1T", 0), ("S1", 2),
            ("P1T", 1), ("PV1", 0), ("S1", 3), ("P1T", 2), ("PV1", 1), ("NIN", 0), ("P1T", 3), ("NIN", 1),
            ("PV1", 2), ("NIN", 2), ("NIN", 3), ("PV1", 3)]


NIN_BANKS = (3, 0, 3, 1)


def plan_banks():
    uses = {k: [] for k in (0, 1, 2, 3, 4, 6)}

    def give(bank, step):
        uses[bank].append(step)

    n = m = 0
    for step in order_mid(False, True):
        if step[0] == "IN":
            give((1, 3)[step[1] % 2], step)
        elif step[0] in ("Q", "K", "KS", "VS", "V"):
            give(n % 2, step)
            n += 1
        elif step[0] == "SMAX":
            give((4, 6)[m % 2], step)
            m += 1
        elif step[0] in ("MROW", "SROW"):
            give({"MROW": 4, "SROW": 6}[step[0]], step)
    for g in range(NG):
        give(3, ("SELF", g))
    for g in range(NG):
        give(2, ("NORMS", g))
        give(3, ("SELFW", g))
        give(g % 2, ("PV", g))
        for k in range(NT):
            give(4, ("ST", g, k, 0))
            give(6, ("ST", g, k, 1))
    give(2, ("PREPB",))
    give(3, ("PREPA",))
    ring = {"X1T": (0, 1), "P1T": (0, 1), "S1": (2, 3), "PV1": (4, 6), "NIN": NIN_BANKS}
    for t in range(NT):
        give((4, 6)[t // 2], ("WO", t))
    for step in ORDER_L1:
        if step[0] in ring:
            give(ring[step[0]][step[1] % len(ring[step[0]])], step)
    for step in order_mid(True, False):
        if step[0] not in ("NORM", "SCALE", "SQ"):
            give(2, step)
    where = {step: (k, c) for k, steps in uses.items() for c, step in enumerate(steps)}
    return where, {k: len(steps) for k, steps in uses.items()}


WHERE, USES = plan_banks()
BEFORE = {k: NIN_BANKS.count(k) + (k == 2) for k in USES}


def build_program(nc, x, f, len_, stage_, lang_, rlang_, Wq, bq, Wk, bk, Wv, bv, Wo, bo, b_prev, b_self,
                  embed, W1, b1, W2, b2, gamma, beta, lora_A, lora_B, lang_embed, out):
    ctx = ExitStack()
    with ctx:
        def sb(name, shape, dt=F32):
            return ctx.enter_context(nc.sbuf_tensor(name, shape, dt))

        def sem(name):
            return ctx.enter_context(nc.semaphore(name))

        ident = sb("ident", [P, P])
        w_hi = sb("w_hi", [P, 4, ND, D], F16)
        w_lo = sb("w_lo", [P, 4, ND, D], F16)
        vecs = sb("vecs", [20, P])
        cols = sb("cols", [P, 20])
        bias_q = sb("bias_q", [P, NG])
        bias_k = sb("bias_k", [P, NG])
        bias_ks = sb("bias_ks", [P, NG])
        bo_rows = sb("bo_rows", [P, D])
        head_cols = sb("head_cols", [P, NG, H])
        head_rows = sb("head_rows", [NROWS, NG, P], F16)
        tiles_in = sb("tiles_in", [P, NT, D])
        xT = sb("xT", [P, 2, ND, S], F16)
        fT = sb("fT", [P, 2, ND, S], F16)
        f16 = sb("f16", [P, 2, NT, D], F16)
        qk32 = sb("qk32", [P, 3, S])
        half = sb("half", [P, 2, 4, S], F16)
        prod = sb("prod", [P, S])
        KQ = sb("KQ", [P, NJ, NG, 2, S], F16)
        V = sb("V", [P, NT, D])
        vsT = sb("vsT", [P, NG, S])
        nmx = sb("nmx", [P, NT, H])
        esum = sb("esum", [P, NT, H])
        self2 = sb("self2", [H, 2, S])
        norms16 = sb("norms16", [NROWS, 2, S], F16)
        shift = sb("shift", [H, S], F16)
        big = sb("big", [P, 2, NJ, S])
        t1 = sb("t1", [P, S])
        t2 = sb("t2", [P, S])
        x1 = sb("x1", [P, NT, D])
        ecol = sb("ecol", [P, 4 + 4 * RANK])
        q1 = sb("q1", [P, 2, D])
        q1T = sb("q1T", [P, 2, 2, ND, P], F16)
        p1_both = sb("p1_both", [P, 2, 2, S])
        nmax = sb("nmax", [P, 2])
        rsum = sb("rsum", [P, 2])
        rrec = sb("rrec", [P, NT])
        hT = sb("hT", [P, 2, P])
        y = sb("y", [P, 2, D])
        st = sb("st", [P, 2, 8])
        lowT = sb("lowT", [RANK + 1, 2, P])
        w1 = sb("w1", [P, ND, A])
        w2 = sb("w2", [P, D])
        b1c = sb("b1c", [P, 1])
        b2r = sb("b2r", [P, D])
        gr = sb("gr", [P, D])
        br = sb("br", [P, D])
        small = sb("small", [RANK, D])
        smallb = sb("smallb", [P, ND, RANK])
        erow = sb("erow", [NT, P])
        lowB = sb("lowB", [RANK + 1, D])
        idx = sb("idx", [1, 4 * B], I32)
        lens_i = sb("lens_i", [B, 1], I32)
        lens_f = sb("lens_f", [B, 1])
        aT = xT
        p1 = p1_both[:, 0]
        p1T = p1_both[:, 1].bitcast(F16).rearrange("p a (h k n) -> p a h k n", h=2, k=NT)
        spread = p1_both[:].rearrange("p a b n -> p (a b) n")
        norms = q1[0:H]
        head_rows32 = t2[0:NROWS, :].rearrange("p (g n) -> p g n", g=NG)
        W_ORDER = (1, 0, 2, 3)
        x2T, xb, x3T, junk = big[:, 0, 0:2], big[:, 0, 2:4], big[:, 1, 0:2], big[:, 1, 2:4]
        stage32 = [big[:, n].rearrange("p a n -> p (a n)") for n in range(2)]
        stage32 = [s_.rearrange("p (a n) -> p a n", a=ND) for s_ in stage32]
        kpos = t1[0:B, :]
        mask16 = half[0:B, 0, 0, :]
        mask_dram = nc.dram_tensor("mask_rows", (B, S), F16, kind="Internal").ap()

        lone = {k: ctx.enter_context(nc.psum_tensor(f"bank{k}", [P, 512], F32)) for k in range(4)}
        pair = {k: ctx.enter_context(nc.psum_tensor(f"banks{k}", [P, 2, 512], F32)) for k in (4, 6)}
        full = {k: sem(f"full{k}") for k in USES}
        free = {k: sem(f"free{k}") for k in USES}

        def bank(step):
            k = WHERE[step][0]
            return lone[k] if k < 4 else pair[k]

        def wait_free(eng, step, b):
            k, c = WHERE[step]
            eng.wait_ge(free[k], b * USES[k] + (BEFORE[k] + c))

        def wait_full(eng, step, b):
            k, c = WHERE[step]
            eng.wait_ge(full[k], b * USES[k] + (BEFORE[k] + c + 1))

        def wait_read(eng, step, b):
            k, c = WHERE[step]
            eng.wait_ge(free[k], b * USES[k] + (BEFORE[k] + c + 1))

        def done(step):
            return full[WHERE[step][0]]

        def read(step):
            return free[WHERE[step][0]]

        vec_in = sem("vec_in")
        bo_in = sem("bo_in")
        idx_in = sem("idx_in")
        len_in = sem("len_in")
        w_in = [sem("w_in0"), sem("w_in1")]
        consts = sem("consts")
        sel_ready = sem("sel_ready")
        rows_ready = sem("rows_ready")
        stack_rows = sem("stack_rows")
        w_hi_done = sem("w_hi_done")
        w_lo_done = sem("w_lo_done")
        bias_row = sem("bias_row")
        sums_done = sem("sums_done")
        bias_full = sem("bias_full")
        bias_done = sem("bias_done")
        len_cast = sem("len_cast")
        mask_made = sem("mask_made")
        mask_out = sem("mask_out")
        tile_in = [sem(f"tile_in{n}") for n in range(NT)]
        in_hi = sem("in_hi")
        f_hi = sem("f_hi")
        f_lo = sem("f_lo")
        qk_hi = sem("qk_hi")
        qk_lo = sem("qk_lo")
        stacked = [sem(f"stacked{g}") for g in range(NG)]
        mask_in = sem("mask_in")
        shift_in = sem("shift_in")
        max_done = sem("max_done")
        MAXIMA = H * NT
        self_neg = sem("self_neg")
        self_diff = sem("self_diff")
        self_exp = sem("self_exp")
        den = sem("den")
        norms_done = sem("norms_done")
        norms_hi = sem("norms_hi")
        norms_lo = sem("norms_lo")
        pv_done = sem("pv_done")
        att_f32 = sem("att_f32")
        att_hi = sem("att_hi")
        att_lo = sem("att_lo")
        x_in = sem("x_in")
        prep_in = sem("prep_in")
        emb_in = sem("emb_in")
        par_in = sem("par_in")
        x_bo = sem("x_bo")
        q1_done = sem("q1_done")
        q1_hi = sem("q1_hi")
        max1 = sem("max1")
        exp1 = sem("exp1")
        sum1 = sem("sum1")
        rec1 = sem("rec1")
        p1_hi = sem("p1_hi")
        xb_done = sem("xb_done")
        xg_done = sem("xg_done")
        mean_done = sem("mean_done")
        sq_done = sem("sq_done")
        newton = sem("newton")
        normed = sem("normed")
        scaled = sem("scaled")
        x3_done = sem("x3_done")
        stored = sem("stored")

        def wait_used(eng, n, i):
            g, k = divmod(n, NT)
            if k == NT - 1:
                wait_full(eng, ("PV", g), i)
            else:
                eng.wait_ge(pv_done, i * NG * (NT - 1) + g * (NT - 1) + k + 1)

        in_loop = nc.Block()
        block = ctx.enter_context(in_loop)

        def hi_lo(eng, out_ap, left, right, first=True, last=True, part=None):
            pairs = [(l[lh], r[rh]) for l, r in zip(left, right) for lh, rh in ((0, 0), (1, 0), (0, 1))]
            each = len(pairs) // PARTS
            at = range(len(pairs)) if part is None else range(part * each, (part + 1) * each)
            for n in at:
                mm = eng.matmul(out_ap, pairs[n][0], pairs[n][1], start=(first and n == 0),
                                stop=(last and n == len(pairs) - 1))
            return mm

        @block.gpsimd
        def _(eng):
            eng.memset(ident[:, :], 0.0).then_inc(consts, 1)
            eng.memset(head_cols[:, :, :], 0.0).then_inc(consts, 1)
            eng.memset(head_rows32[:, :, :], 0.0).then_inc(consts, 1)
            eng.wait_ge(consts, 3)
            eng.affine_select(out=ident[:, :], in_=ident[:, :], compare_op=ALU.not_equal, fill=1.0,
                              base=0, pattern=[[-1, P]], channel_multiplier=1).then_inc(sel_ready, 1)
            for n, low in enumerate((0, LOW_ROW)):
                for g in range(NG):
                    v = head_rows32[:, g, :].rearrange("h (j d) -> h j d", j=NJ)
                    eng.wait_ge(sel_ready, 1 + NG * n + g)
                    eng.affine_select(out=v, in_=v, compare_op=ALU.not_equal, fill=1.0 / RS, base=-g - low,
                                      pattern=[[-NG, NJ], [0, DH]], channel_multiplier=1).then_inc(sel_ready, 1)
            eng.wait_ge(sel_ready, 1 + 2 * NG)
            eng.iota(kpos, pattern=[[1, S]], base=0, channel_multiplier=0,
                     allow_small_or_imprecise_dtypes=True).then_inc(sel_ready, 1)
            eng.wait_ge(sel_ready, 2 + 2 * NG)
            eng.memset(KQ[MASK_ROW:P, :, :, 1, :], BIG).then_inc(stack_rows, 1)
            eng.wait_ge(stack_rows, 1)
            eng.memset(KQ[MASK_ROW:P, :, :, 0, :], 1.0).then_inc(stack_rows, 1)
            eng.wait_ge(stack_rows, 2)

            def mid(tail, head, i):
                b = i + 1 if tail else i
                for step in order_mid(tail, head):
                    if step[0] == "IN":
                        n = step[1] - NT
                        eng.wait_ge(f_hi, b * NT + n + 1)
                        eng.tensor_tensor(f16[:, 1, n, :], tiles_in[:, n, :], f16[:, 0, n, :], ALU.subtract
                                          ).then_inc(f_lo, 1)
                    elif step[0] == "HALF":
                        g, k = step[2], int(step[1] == "K")
                        eng.wait_ge(qk_hi, b * 2 * NG + 2 * g + 2 - k)
                        hi = 0 if k else 2
                        eng.tensor_tensor(half[:, g % 2, hi + 1, :], qk32[:, 2 if k else g % 2, :],
                                          half[:, g % 2, hi, :], ALU.subtract).then_inc(qk_lo, 1)
                    elif step[0] == "X2T":
                        t = step[1]
                        if t >= 2:
                            wait_read(eng, ("ADP", t - 2), i)
                        else:
                            wait_used(eng, NSTEP - 1, i)
                        if t == 0:
                            eng.wait_ge(par_in, i * 96 + 96)
                        wait_read(eng, ("PV1", t), i)
                        eng.tensor_tensor(xb[:, t % 2, :], x1[:, t, :], b2r[:, :], ALU.add).then_inc(xb_done, 1)
                    elif step[0] == "NORM" and step[2] == 0:
                        for t in (step[1], step[1] + 1):
                            wait_full(eng, ("X2T", t), i)
                            eng.wait_ge(xb_done, i * NT + t + 1)
                            eng.tensor_tensor(x1[:, t, :], x1[:, t, :], br[:, :], ALU.add).then_inc(xg_done, 1)
                    elif step[0] == "SCALE":
                        t = step[1]
                        eng.wait_ge(normed, i * NT + t + 1)
                        eng.tensor_tensor(y[:, t % 2, :], y[:, t % 2, :], gr[:, :], ALU.mult).then_inc(scaled, 1)
                        eng.wait_ge(scaled, i * NT + t + 1)
                        eng.wait_ge(xg_done, i * NT + t + 1)
                        eng.tensor_tensor(x1[:, t, :], y[:, t % 2, :], x1[:, t, :], ALU.add).then_inc(x3_done, 1)

            def add_bo(i):
                eng.wait_ge(x_in, i * 16 + 16)
                for t in range(NT):
                    eng.tensor_tensor(x1[:, t, :], x1[:, t, :], bo_rows[:, :], ALU.add).then_inc(x_bo, 1)

            eng.wait_ge(bo_in, 16)
            mid(False, True, 0)
            with eng.Fori(0, B - 1) as i:
                add_bo(i)
                mid(True, True, i)
            add_bo(B - 1)
            mid(True, False, B - 1)

        @block.sync
        def _(eng):
            def load_weight(n):
                w = (Wk, Wq, Wv, Wo)[n]
                eng.dma_start(stage32[n % 2], w.rearrange("(t p) n -> p t n", p=P)).then_inc(w_in[n % 2], 16)

            def load_tile(n, b):
                src = x if n < NT else f
                t = n % NT
                if isinstance(b, int):
                    rows = src[b, t * P:(t + 1) * P, :]
                else:
                    rows = src[bass.ds(b, 1), t * P:(t + 1) * P, :].rearrange("a p n -> (a p) n")
                eng.dma_start(tiles_in[:, t, :], rows).then_inc(tile_in[t], 16)

            def whole(src, b):
                if isinstance(b, int):
                    return src[b].rearrange("(t p) n -> p t n", p=P)
                return src[bass.ds(b, 1), :, :].rearrange("a (t p) n -> p (a t) n", p=P)

            def mid(tail, head, i):
                b = i + 1 if tail else i
                for step in order_mid(tail, head):
                    if step[0] == "HALF":
                        g, k = step[2], int(step[1] == "K")
                        if g == 0 and k:
                            row = mask_dram[bass.ds(b, 1), :] if tail else mask_dram[b:b + 1, :]
                            if tail:
                                wait_full(eng, ("ST", NG - 1, NT - 1, 1), i)
                            else:
                                eng.wait_ge(stack_rows, 2)
                            eng.dma_start(KQ[MASK_ROW:MASK_ROW + 1, :, :, 0, :].rearrange("o j g n -> o (j g) n"),
                                          row.to_broadcast([H, S]).rearrange("(o h) n -> o h n", o=1)
                                          ).then_inc(mask_in, 16)
                        if not k:
                            eng.wait_ge(qk_lo, b * 2 * NG + 2 * g + 2)
                            for r, parts in enumerate((slice(0, 3, 2), slice(1, 3), slice(0, 4, 3))):
                                for j in range(NJ):
                                    eng.dma_start(KQ[r * DH:(r + 1) * DH, j, g, :, :],
                                                  half[j * DH:(j + 1) * DH, g % 2, parts, :]
                                                  ).then_inc(stacked[g], 16)
                    elif step[0] == "MROW":
                        wait_read(eng, step, b)
                        eng.dma_start(KQ[SHIFT_ROW:SHIFT_ROW + 1, :, :, 1, :].rearrange("o j g n -> o (j g) n"),
                                      shift[:, :]).then_inc(shift_in, 16)
                    elif step[0] == "LORA":
                        t = step[1]
                        wait_read(eng, step, i)
                        if isinstance(i, int):
                            dst = out[i, t * P:(t + 1) * P, :]
                        else:
                            dst = out[bass.ds(i, 1), t * P:(t + 1) * P, :].rearrange("a p n -> (a p) n")
                        eng.dma_start(dst, x1[:, t, :]).then_inc(stored, 16)

            def params(i):
                stage = eng.value_load(idx[0:1, bass.ds(i, 1)], min_val=0, max_val=STAGES - 1)
                lang = eng.value_load(idx[0:1, bass.ds(i + B, 1)], min_val=0, max_val=LANGS - 1)
                rlang = eng.value_load(idx[0:1, bass.ds(i + 2 * B, 1)], min_val=0, max_val=RLANGS - 1)
                wait_read(eng, ("SROW",), i)
                eng.dma_start(x1[:, :, :], whole(x, i)).then_inc(x_in, 16)
                eng.dma_start(erow[:, :], embed[bass.ds(stage, 1), :].rearrange("a (t p) -> (a t) p", p=P)
                              ).then_inc(prep_in, 16)
                eng.dma_start(small[:, :], lora_A[bass.ds(rlang, 1), :, :].rearrange("a r n -> (a r) n")
                              ).then_inc(prep_in, 16)
                eng.dma_start(smallb[:, :, :], lora_B[bass.ds(rlang, 1), :, :].rearrange("a (t p) r -> p (a t) r", p=P)
                              ).then_inc(prep_in, 16)
                eng.dma_start(lowB[RANK:RANK + 1, :], lang_embed[bass.ds(rlang, 1), :]).then_inc(emb_in, 16)
                eng.dma_start(w1[:, :, :], W1[bass.ds(lang, 1), :, :].rearrange("a (t p) n -> p (a t) n", p=P)
                              ).then_inc(par_in, 16)
                eng.dma_start(w2[:, :], W2[bass.ds(lang, 1), :, :].rearrange("a p n -> (a p) n")).then_inc(par_in, 16)
                eng.dma_start(b1c[:, :], b1[bass.ds(lang, 1), :].rearrange("a (p o) -> (a p) o", o=1)
                              ).then_inc(par_in, 16)
                for dst, src in ((b2r, b2), (gr, gamma), (br, beta)):
                    eng.dma_start(dst[:, :], src[bass.ds(lang, 1), :].to_broadcast([P, D])).then_inc(par_in, 16)

            def swap_tiles(i):
                for n in range(NT):
                    wait_full(eng, ("NIN", n), i)
                    load_tile(n + NT, i + 1)

            def prefetch(i):
                for t in range(NT):
                    eng.wait_ge(f_lo, i * NT + t + 1)
                    load_tile(t, i + 1)

            load_weight(0)
            for n, v in enumerate((bq, bk, bv, b_self, b_prev)):
                flat = v if len(v.shape) == 1 else v.rearrange("a c n -> (a c n)")
                eng.dma_start(vecs[4 * n:4 * n + 4, :], flat.rearrange("(t p) -> t p", p=P)).then_inc(vec_in, 16)
            eng.dma_start(lens_i[:, :], len_.rearrange("(n a) -> n a", a=1)).then_inc(len_in, 16)
            for t in range(NT):
                load_tile(t, 0)
            load_weight(1)
            for n, v in enumerate((stage_, lang_, rlang_)):
                eng.dma_start(idx[:, n * B:(n + 1) * B], v.rearrange("(a n) -> a n", a=1)).then_inc(idx_in, 16)
            eng.dma_start(bo_rows[:, :], bo.rearrange("(a n) -> a n", a=1).to_broadcast([P, D])).then_inc(bo_in, 16)
            swap_tiles(-1)
            eng.wait_ge(mask_made, 1)
            eng.dma_start(mask_dram, mask16).then_inc(mask_out, 16)
            for n in (2, 3):
                eng.wait_ge(w_lo_done, n - 1)
                eng.wait_ge(bias_full, 2)
                load_weight(n)
            eng.wait_ge(mask_out, 16)
            eng.wait_ge(idx_in, 48)
            mid(False, True, 0)
            with eng.Fori(0, B - 1) as i:
                params(i)
                prefetch(i)
                swap_tiles(i)
                mid(True, True, i)
            params(B - 1)
            mid(True, False, B - 1)
            eng.wait_ge(stored, B * NT * 16)

        @block.scalar
        def _(eng):
            def weight_high(n):
                eng.wait_ge(w_in[n % 2], 16 * (n // 2 + 1))
                eng.activation(w_hi[:, W_ORDER[n], :, :], stage32[n % 2], ACT.Copy, scale=WS).then_inc(w_hi_done, 1)

            def take_high(step, b, big_t):
                n = step[1] % NT
                wait_full(eng, step, b)
                eng.activation(big_t[:, 0, :, n * P:(n + 1) * P], bank(step)[:, :].rearrange("p (t n) -> p t n", t=ND),
                               ACT.Copy).then_inc(in_hi, 1)

            def mid(tail, head, i):
                b = i + 1 if tail else i
                for step in order_mid(tail, head):
                    kind = step[0]
                    if kind == "IN":
                        take_high(step, b, fT)
                        n = step[1] - NT
                        eng.activation(f16[:, 0, n, :], tiles_in[:, n, :], ACT.Copy).then_inc(f_hi, 1)
                    elif kind in ("Q", "K"):
                        g, k = step[1], int(kind == "K")
                        wait_full(eng, step, b)
                        if k and g >= 1:
                            eng.wait_ge(qk_lo, b * 2 * NG + 2 * g - 1)
                        elif k and tail:
                            eng.wait_ge(qk_lo, b * 2 * NG - 1)
                        elif not k and g >= 2:
                            eng.wait_ge(qk_lo, b * 2 * NG + 2 * g - 2)
                            wait_read(eng, ("KS", g - 2), b)
                        elif not k and tail:
                            eng.wait_ge(qk_lo, i * 2 * NG + 2 * NG - 2 + 2 * g)
                            wait_read(eng, ("KS", NG - 2 + g), i)
                        eng.activation(qk32[:, 2 if k else g % 2, :], bank(step)[:, :], ACT.Identity,
                                       bias=(bias_k if k else bias_q)[:, g:g + 1],
                                       scale=1.0 / WS if k else SCALE / WS).then_inc(read(step), 1)
                    elif kind == "VS":
                        wait_full(eng, step, b)
                        eng.activation(vsT[:, step[1], :], bank(step)[:, :], ACT.Copy, scale=1.0 / WS
                                       ).then_inc(read(step), 1)
                    elif kind == "V":
                        wait_full(eng, step, b)
                        eng.activation(V[:, step[1], :], bank(step)[:, :], ACT.Copy, scale=1.0 / WS
                                       ).then_inc(read(step), 1)
                    elif kind == "SMAX":
                        _, g, u = step
                        t, q = divmod(u, 2)
                        for j in (2 * q, 2 * q + 1):
                            eng.wait_ge(max_done, b * MAXIMA + (g * 2 * NT + u) * 2 + j % 2 + 1)
                            h = NG * j + g
                            ins = eng.activation(bank(step)[:, j % 2, :], bank(step)[:, j % 2, :], ACT.Exp,
                                                 bias=nmx[:, t, h:h + 1], accum_out=esum[:, t, h:h + 1])
                        ins.then_inc(read(step), 1)
                    elif kind == "NEG":
                        wait_full(eng, ("SELF", NG - 1), b)
                        if tail:
                            eng.wait_ge(norms_done, b)
                        eng.activation(self2[:, 0, :], lone[3][0:H, :], ACT.Copy, scale=-1.0
                                       ).then_inc(read(("SELF", 0)), NG)
                    elif kind == "SROW":
                        eng.wait_ge(self_diff, b * 2 + 2)
                        eng.activation(self2[:, :, :], self2[:, :, :], ACT.Exp).then_inc(self_exp, 1)
                    elif kind == "X2T":
                        t = step[1]
                        wait_full(eng, step, i)
                        eng.activation(x2T[:, t % 2, :], lone[2][:, :], ACT.Copy).then_inc(read(step), 1)
                    elif kind == "HID":
                        t = step[1]
                        if t == 0:
                            eng.wait_ge(par_in, i * 96 + 96)
                        wait_full(eng, step, i)
                        eng.activation(hT[:, t % 2, :], lone[2][:, 0:P], ACT.Relu, bias=b1c[:, :]
                                       ).then_inc(read(step), 1)
                    elif kind == "SQ":
                        t = step[1]
                        eng.wait_ge(mean_done, i * NT + t + 1)
                        eng.activation(junk[:, t % 2, :], y[:, t % 2, :], ACT.Square, bias=st[:, t % 2, 1:2],
                                       accum_out=st[:, t % 2, 2:3]).then_inc(sq_done, 1)
                    elif kind == "X3T":
                        t = step[1]
                        wait_full(eng, step, i)
                        eng.activation(x3T[:, t % 2, :], lone[2][:, :], ACT.Copy).then_inc(read(step), 1)
                    elif kind == "LOW":
                        t = step[1]
                        wait_full(eng, step, i)
                        eng.activation(lowT[0:RANK, t % 2, :], lone[2][0:RANK, 0:P], ACT.Copy
                                       ).then_inc(read(step), 1)

            def attention(i):
                wait_free(eng, ("NORMS", 0), i)
                for n in range(NSTEP):
                    g, k = divmod(n, NT)
                    if n >= 2:
                        wait_used(eng, n - 2, i)
                    for u in range(2):
                        step = ("ST", g, k, u)
                        wait_full(eng, step, i)
                        eng.activation(big[:, n % 2, 2 * u:2 * u + 2, :], bank(step)[:, :, :], ACT.Exp
                                       ).then_inc(read(step), 1)
                wait_full(eng, ("PREPB",), i)
                eng.activation(lowB[0:RANK, :], lone[2][0:RANK, :], ACT.Copy).then_inc(read(("PREPB",)), 1)
                wait_full(eng, ("PREPA",), i)
                eng.activation(ecol[:, :], lone[3][:, 0:4 + 4 * RANK], ACT.Copy).then_inc(read(("PREPA",)), 1)

            def layer1(i, head):
                for step in ORDER_L1:
                    kind = step[0]
                    t = step[-1]
                    if kind == "NIN" and head:
                        take_high(step, i, xT)
                    elif kind == "X1T":
                        wait_full(eng, step, i)
                        eng.activation(q1T[:, t % 2, 0, :, :], bank(step)[:, :].rearrange("p (t n) -> p t n", t=ND),
                                       ACT.Copy).then_inc(q1_hi, 1)
                    elif kind == "WO":
                        wait_read(eng, ("PREPA",), i)
                        wait_read(eng, step, i)
                        if t >= 2:
                            wait_full(eng, ("X1T", t - 2), i)
                        eng.activation(q1[:, t % 2, :], x1[:, t, :], ACT.Identity, bias=ecol[:, t:t + 1]
                                       ).then_inc(q1_done, 1)
                    elif kind == "S1":
                        eng.wait_ge(max1, i * NT + t + 1)
                        if t >= 2:
                            wait_full(eng, ("P1T", t - 2), i)
                        eng.activation(p1[:, t % 2, :], bank(step)[:, :], ACT.Exp, bias=nmax[:, t % 2:t % 2 + 1],
                                       accum_out=rsum[:, t % 2:t % 2 + 1]).then_inc(read(step), 1)
                    elif kind == "P1T":
                        wait_full(eng, step, i)
                        if t >= 2:
                            wait_full(eng, ("PV1", t - 2), i)
                        eng.activation(p1T[:, t % 2, 0, :, :], bank(step)[:, :].rearrange("p (t n) -> p t n", t=NT),
                                       ACT.Copy, scale=PS).then_inc(p1_hi, 1)

            weight_high(0)
            for n in range(NT):
                take_high(("NIN", n), -1, xT)
            for n in range(1, 4):
                weight_high(n)
            eng.wait_ge(bias_done, 3)
            mid(False, True, 0)
            with eng.Fori(0, B - 1) as i:
                attention(i)
                layer1(i, True)
                mid(True, True, i)
            attention(B - 1)
            layer1(B - 1, False)
            mid(True, False, B - 1)

        @block.vector
        def _(eng):
            eng.memset(norms16[:, :, :], 0.0).then_inc(rows_ready, 1)
            eng.memset(lowT[:, :, :], 1.0).then_inc(rows_ready, 1)
            eng.wait_ge(consts, 3)
            for j in range(NJ):
                for g in range(NG):
                    eng.memset(head_cols[DH * j:DH * j + DH, g, NG * j + g:NG * j + g + 1], 1.0 / WS
                               ).then_inc(rows_ready, 1)
            eng.wait_ge(full[2], 1)
            eng.tensor_copy(cols[:, :], lone[2][:, 0:20]).then_inc(free[2], 1)
            eng.wait_ge(len_in, 16)
            eng.tensor_copy(lens_f[:, :], lens_i[:, :]).then_inc(len_cast, 1)
            eng.wait_ge(len_cast, 1)
            eng.wait_ge(sel_ready, 2 + 2 * NG)
            eng.tensor_copy(head_rows[:, :, :], head_rows32[:, :, :]).then_inc(rows_ready, 1)
            eng.tensor_scalar(mask16, kpos, lens_f[:, 0:1], -BIG, ALU.is_ge, ALU.mult).then_inc(mask_made, 1)

            def weight_low(n):
                eng.wait_ge(w_hi_done, n + 1)
                eng.scalar_tensor_tensor(out=w_lo[:, W_ORDER[n], :, :], in0=stage32[n % 2], scalar=WS,
                                         in1=w_hi[:, W_ORDER[n], :, :], op0=ALU.mult, op1=ALU.subtract
                                         ).then_inc(w_lo_done, 1)

            def bias_rows(n):
                eng.wait_ge(bias_full, n + 1)
                eng.tensor_copy(q1[0:2 - n, n, :], pair[4 + 2 * n][0:2 - n, 0, :]).then_inc(bias_row, 1)

            def biases():
                of_k = pair[4][:, 1, 0:2 * NG].rearrange("p (g v) -> p v g", v=2)
                eng.wait_ge(free[2], 1)
                eng.wait_ge(bias_full, 4)
                eng.tensor_tensor(bias_k[:, :], of_k[:, 1, :], cols[:, 4:8], ALU.add).then_inc(bias_done, 1)
                eng.tensor_tensor(t2[:, 0:4], pair[6][:, 1, 0:NG], cols[:, 0:4], ALU.add).then_inc(sums_done, 1)
                eng.tensor_tensor(t2[:, 4:8], of_k[:, 0, :], cols[:, 4:8], ALU.add).then_inc(sums_done, 1)
                eng.wait_ge(sums_done, 2)
                eng.tensor_scalar(bias_q[:, :], t2[:, 0:4], SCALE, None, ALU.mult).then_inc(bias_done, 1)
                eng.tensor_scalar(bias_ks[:, :], t2[:, 4:8], WS, None, ALU.mult).then_inc(bias_done, 1)

            def take_low(step, b, big_t, high_count):
                n = step[1] % NT
                at = slice(n * P, (n + 1) * P)
                eng.wait_ge(in_hi, high_count)
                eng.tensor_tensor(big_t[:, 1, :, at], bank(step)[:, :].rearrange("p (t n) -> p t n", t=ND),
                                  big_t[:, 0, :, at], ALU.subtract).then_inc(read(step), 1)

            def norm_piece(t, piece, i):
                si = st[:, :, :].bitcast(I32)
                var, r, c, c_int, r_int = st[:, :, 3], st[:, :, 4], st[:, :, 5], si[:, :, 5], si[:, :, 4]
                base = i * (NT // 2 * NEWTON) + t // 2 * NEWTON
                each = NEWTON // (NORM_PIECES - 1)
                for n in range(piece * each, min(piece * each + each, NEWTON)):
                    if n == 0:
                        eng.wait_ge(sq_done, i * NT + t + 2)
                    else:
                        eng.wait_ge(newton, base + n)
                    if n == 0:
                        op = eng.tensor_scalar(var, st[:, :, 2], 1.0 / D, EPS, ALU.mult, ALU.add)
                    elif n == 1:
                        op = eng.tensor_scalar(c_int, si[:, :, 3], 1, None, ALU.logical_shift_right)
                    elif n == 2:
                        op = eng.tensor_scalar(r_int, c_int, -1, 0x5F3759DF, ALU.mult, ALU.add)
                    elif n % 4 == 3:
                        op = eng.tensor_tensor(c, r, r, ALU.mult)
                    elif n % 4 == 0:
                        op = eng.tensor_tensor(c, c, var, ALU.mult)
                    elif n % 4 == 1:
                        op = eng.tensor_scalar(c, c, -0.5, 1.5, ALU.mult, ALU.add)
                    else:
                        op = eng.tensor_tensor(r, r, c, ALU.mult)
                    op.then_inc(newton, 1)
                if piece == NORM_PIECES - 1:
                    eng.wait_ge(newton, base + NEWTON)
                    for n in range(2):
                        eng.tensor_scalar(y[:, n, :], y[:, n, :], st[:, n, 1:2], st[:, n, 4:5], ALU.add, ALU.mult
                                          ).then_inc(normed, 1)

            def mid(tail, head, i):
                b = i + 1 if tail else i
                for step in order_mid(tail, head):
                    kind = step[0]
                    if kind == "IN":
                        take_low(step, b, fT, b * 2 * NT + step[1] + 1)
                    elif kind == "HALF":
                        g, k = step[2], int(step[1] == "K")
                        wait_read(eng, step[1:], b)
                        if g >= 2:
                            eng.wait_ge(stacked[g - 2], b * DMAS_PER_STACK + DMAS_PER_STACK)
                        elif tail:
                            eng.wait_ge(stacked[NG - 2 + g], i * DMAS_PER_STACK + DMAS_PER_STACK)
                        eng.tensor_copy(half[:, g % 2, 0 if k else 2, :], qk32[:, 2 if k else g % 2, :]
                                        ).then_inc(qk_hi, 1)
                    elif kind == "KS":
                        g = step[1]
                        wait_full(eng, step, b)
                        if g >= 1:
                            wait_full(eng, ("SELF", g - 1), b)
                        elif tail:
                            wait_full(eng, ("SELF", NG - 1), i)
                        eng.scalar_tensor_tensor(out=prod[:, :], in0=bank(step)[:, :], scalar=bias_ks[:, g:g + 1],
                                                 in1=qk32[:, g % 2, :], op0=ALU.add, op1=ALU.mult
                                                 ).then_inc(read(step), 1)
                    elif kind == "SMAX":
                        _, g, u = step
                        t, q = divmod(u, 2)
                        wait_full(eng, step, b)
                        for j in (2 * q, 2 * q + 1):
                            h = NG * j + g
                            eng.tensor_reduce(nmx[:, t, h:h + 1], bank(step)[:, j % 2, :], AX_X, ALU.max,
                                              negate=True).then_inc(max_done, 1)
                    elif kind == "MROW":
                        wait_full(eng, step, b)
                        wait_read(eng, ("SELF", NG - 1), b)
                        if tail:
                            eng.wait_ge(shift_in, b * 16)
                        eng.tensor_tensor(shift[:, :], bank(step)[0:H, 0, :], self2[:, 0, :], ALU.min
                                          ).then_inc(self_neg, 1)
                        eng.wait_ge(self_neg, b + 1)
                        eng.tensor_tensor(self2[:, 1, :], shift[:, :], bank(step)[0:H, 0, :], ALU.subtract
                                          ).then_inc(read(step), 1)
                        eng.tensor_tensor(self2[:, 0, :], shift[:, :], self2[:, 0, :], ALU.subtract
                                          ).then_inc(self_diff, 2)
                    elif kind == "SROW":
                        wait_full(eng, step, b)
                        eng.wait_ge(self_exp, b + 1)
                        if tail:
                            eng.wait_ge(stored, b * NT * 16)
                        eng.tensor_tensor(norms[:, 0, :], bank(step)[0:H, 0, :], self2[:, 1, :], ALU.mult
                                          ).then_inc(read(step), 1)
                        wait_read(eng, step, b)
                        eng.tensor_tensor(norms[:, 0, :], norms[:, 0, :], self2[:, 0, :], ALU.add).then_inc(den, 1)
                        eng.wait_ge(den, b * 2 + 1)
                        eng.reciprocal(norms[:, 0, :], norms[:, 0, :]).then_inc(den, 1)
                        eng.wait_ge(den, b * 2 + 2)
                        eng.tensor_tensor(norms[:, 1, :], norms[:, 0, :], self2[:, 0, :], ALU.mult
                                          ).then_inc(norms_done, 1)
                        eng.wait_ge(norms_done, b + 1)
                        eng.tensor_scalar(norms16[0:H, :, :], norms[:, :, :], RS, None, ALU.mult).then_inc(norms_hi, 1)
                        eng.wait_ge(norms_hi, b + 1)
                        eng.scalar_tensor_tensor(out=norms16[LOW_ROW:NROWS, :, :], in0=norms[:, :, :], scalar=RS,
                                                 in1=norms16[0:H, :, :], op0=ALU.mult, op1=ALU.subtract
                                                 ).then_inc(norms_lo, 1)
                    elif kind == "ADP":
                        t = step[1]
                        wait_full(eng, step, i)
                        eng.wait_ge(xb_done, i * NT + t + 1)
                        if t >= 2:
                            eng.wait_ge(x3_done, i * NT + t - 1)
                        eng.scalar_tensor_tensor(out=y[:, t % 2, :], in0=lone[2][:, :], scalar=1.0,
                                                 in1=xb[:, t % 2, :], op0=ALU.mult, op1=ALU.add,
                                                 accum_out=st[:, t % 2, 0:1]).then_inc(read(step), 1)
                        wait_read(eng, step, i)
                        eng.tensor_scalar(st[:, t % 2, 1:2], st[:, t % 2, 0:1], -1.0 / D, None, ALU.mult
                                          ).then_inc(mean_done, 1)
                    elif kind == "NORM":
                        norm_piece(step[1], step[2], i)
                    elif kind == "LORA":
                        t = step[1]
                        wait_full(eng, step, i)
                        eng.tensor_tensor(x1[:, t, :], lone[2][:, :], x1[:, t, :], ALU.add
                                          ).then_inc(read(step), 1)

            def take_norms(g, i):
                wait_full(eng, ("NORMS", g), i)
                eng.tensor_copy(spread[:, g, :], lone[2][:, :]).then_inc(read(("NORMS", g)), 1)
                wait_full(eng, ("SELFW", g), i)
                wait_read(eng, ("VS", g), i)
                eng.tensor_tensor(vsT[:, g, :], lone[3][:, :], vsT[:, g, :], ALU.mult
                                  ).then_inc(read(("SELFW", g)), 1)

            def finish_group(g, i):
                wait_full(eng, ("PV", g), i)
                wait_read(eng, ("NORMS", g), i)
                eng.tensor_tensor(t1[:, :], bank(("PV", g))[:, :], spread[:, g, :], ALU.mult
                                  ).then_inc(read(("PV", g)), 1)
                wait_read(eng, ("PV", g), i)
                wait_read(eng, ("SELFW", g), i)
                eng.tensor_tensor(t2[:, :], t1[:, :], vsT[:, g, :], ALU.add).then_inc(att_f32, 1)
                eng.wait_ge(att_f32, i * NG + g + 1)
                eng.tensor_scalar(aT[:, 0, g, :], t2[:, :], cols[:, 8 + g:9 + g], None, ALU.add).then_inc(att_hi, 1)
                eng.wait_ge(att_hi, i * NG + g + 1)
                eng.scalar_tensor_tensor(out=aT[:, 1, g, :], in0=t2[:, :], scalar=cols[:, 8 + g:9 + g],
                                         in1=aT[:, 0, g, :], op0=ALU.add, op1=ALU.subtract).then_inc(att_lo, 1)

            def attention(i):
                take_norms(0, i)
                for g in range(NG):
                    if g < 2:
                        take_norms(2 * g + 1, i)
                    finish_group(g, i)
                    if g < 1:
                        take_norms(2, i)

            def layer1(i, head):
                for step in ORDER_L1:
                    kind, t = step[0], step[-1]
                    if kind == "NIN" and head:
                        take_low(step, i, xT, i * 2 * NT + (2 * NT + t + 1))
                    elif kind == "WO":
                        eng.wait_ge(x_bo, i * NT + t + 1)
                        wait_full(eng, step, i)
                        eng.scalar_tensor_tensor(out=x1[:, t, :], in0=bank(step)[:, t % 2, :], scalar=1.0 / WS,
                                                 in1=x1[:, t, :], op0=ALU.mult, op1=ALU.add
                                                 ).then_inc(read(step), 1)
                    elif kind == "X1T":
                        eng.wait_ge(q1_hi, i * NT + t + 1)
                        eng.tensor_tensor(q1T[:, t % 2, 1, :, :], bank(step)[:, :].rearrange("p (t n) -> p t n", t=ND),
                                          q1T[:, t % 2, 0, :, :], ALU.subtract).then_inc(read(step), 1)
                    elif kind == "S1":
                        wait_full(eng, step, i)
                        if t >= 2:
                            wait_read(eng, ("S1", t - 2), i)
                        eng.tensor_reduce(nmax[:, t % 2:t % 2 + 1], bank(step)[:, :], AX_X, ALU.max,
                                          negate=True).then_inc(max1, 1)
                    elif kind == "P1T":
                        wait_read(eng, ("S1", t), i)
                        eng.tensor_scalar(rrec[:, t:t + 1], rsum[:, t % 2:t % 2 + 1], PS, None, ALU.mult
                                          ).then_inc(sum1, 1)
                        eng.wait_ge(sum1, i * NT + t + 1)
                        eng.reciprocal(rrec[:, t:t + 1], rrec[:, t:t + 1]).then_inc(rec1, 1)
                        eng.wait_ge(p1_hi, i * NT + t + 1)
                        eng.scalar_tensor_tensor(out=p1T[:, t % 2, 1, :, :],
                                                 in0=bank(step)[:, :].rearrange("p (t n) -> p t n", t=NT), scalar=PS,
                                                 in1=p1T[:, t % 2, 0, :, :], op0=ALU.mult, op1=ALU.subtract
                                                 ).then_inc(read(step), 1)
                    elif kind == "PV1":
                        eng.wait_ge(rec1, i * NT + t + 1)
                        wait_full(eng, step, i)
                        eng.wait_ge(q1_done, i * NT + t + 1)
                        eng.scalar_tensor_tensor(out=x1[:, t, :], in0=bank(step)[:, 0, :],
                                                 scalar=rrec[:, t:t + 1], in1=x1[:, t, :],
                                                 op0=ALU.mult, op1=ALU.add).then_inc(read(step), 1)

            weight_low(0)
            bias_rows(0)
            for n in range(NT):
                take_low(("NIN", n), -1, xT, n + 1)
            weight_low(1)
            bias_rows(1)
            biases()
            for n in (2, 3):
                weight_low(n)
            eng.wait_ge(bias_done, 3)
            eng.wait_ge(mask_out, 16)
            mid(False, True, 0)
            with eng.Fori(0, B - 1) as i:
                attention(i)
                layer1(i, True)
                mid(True, True, i)
            attention(B - 1)
            layer1(B - 1, False)
            mid(True, False, B - 1)

        @block.tensor
        def _(eng):
            eng.wait_ge(sel_ready, 1)
            eng.wait_ge(vec_in, 5 * 16)
            eng.transpose(lone[2][:, 0:20], vecs[:, :], ident[0:20, 0:20]).then_inc(full[2], 1)

            def vector_rows(n):
                eng.wait_ge(w_in[n], 16)
                for d in range(ND):
                    mm = eng.matmul(pair[4 + 2 * n][0:2 - n, 0, :], cols[:, 12 + d:(17 if n == 0 else 13) + d:4],
                                    stage32[n][:, d, :], start=(d == 0), stop=(d == ND - 1))
                mm.then_inc(bias_full, 1)

            def vector_cols(n):
                eng.wait_ge(bias_row, n + 1)
                m = 2 - n
                for g in range(NG):
                    mm = eng.transpose(pair[4 + 2 * n][:, 1, m * g:m * g + m], q1[0:m, n, g * P:(g + 1) * P],
                                       ident[0:m, 0:m])
                mm.then_inc(bias_full, 1)

            def weights(w, d, n):
                at = slice(n * P, (n + 1) * P)
                return w_hi[:, w, d, at], w_lo[:, w, d, at]

            def transpose4(step, src, signal):
                for d in range(4):
                    mm = eng.transpose(bank(step)[:, d * P:(d + 1) * P], src[:, d * P:(d + 1) * P], ident[:, :])
                mm.then_inc(signal, 1)

            def project(step, part, b):
                kind, g = step
                if part == 0:
                    if step == ("VS", 0) and isinstance(b, int):
                        eng.wait_ge(w_lo_done, 4)
                    if step == ("Q", 0):
                        wait_read(eng, ("IN", 2 * NT - 2), b)
                        wait_read(eng, ("IN", 2 * NT - 1), b)
                    wait_free(eng, step, b)
                if kind == "V":
                    at = slice(g * P, (g + 1) * P)
                    left = [(xT[:, 0, d, at], xT[:, 1, d, at]) for d in range(ND)]
                    right = [(w_hi[:, 2, d, :], w_lo[:, 2, d, :]) for d in range(ND)]
                else:
                    src = xT if kind == "K" else fT
                    left = [weights({"Q": 0, "K": 1, "KS": 1, "VS": 2}[kind], d, g) for d in range(ND)]
                    right = [(src[:, 0, d, :], src[:, 1, d, :]) for d in range(ND)]
                return hi_lo(eng, bank(step)[:, :], left, right, part=part)

            def mid(tail, head, i):
                b = i + 1 if tail else i
                for step in order_mid(tail, head):
                    kind = step[0]
                    if kind == "IN":
                        n = step[1] - NT
                        eng.wait_ge(tile_in[n], b * 32 + 32)
                        wait_free(eng, step, b)
                        transpose4(step, tiles_in[:, n, :], done(step))
                    elif kind == "PART":
                        project(step[2], step[1], b)
                    elif kind in ("Q", "K", "KS", "VS", "V"):
                        project(step, PARTS - 1, b).then_inc(done(step), 1)
                    elif kind == "SELF":
                        g = step[1]
                        if g == 0 and not tail:
                            eng.wait_ge(rows_ready, 3 + H)
                        if g == 0:
                            wait_free(eng, step, b)
                        wait_read(eng, ("KS", g), b)
                        eng.matmul(lone[3][0:H, :], head_cols[:, g, :], prod[:, :], start=(g == 0),
                                   stop=(g == NG - 1), skip_group_check=True).then_inc(done(step), 1)
                    elif kind == "SMAX":
                        _, g, u = step
                        t, q = divmod(u, 2)
                        if u == 0:
                            eng.wait_ge(stacked[g], b * DMAS_PER_STACK + DMAS_PER_STACK)
                            if g == 0:
                                eng.wait_ge(mask_in, b * 16 + 16)
                        wait_free(eng, step, b)
                        for j in (2 * q, 2 * q + 1):
                            mm = eng.matmul(bank(step)[:, j % 2, :], KQ[0:SHIFT_ROW, j, g, 1, t * P:(t + 1) * P],
                                            KQ[0:SHIFT_ROW, j, g, 0, :], start=True, stop=True)
                        mm.then_inc(done(step), 1)
                    elif kind == "MROW":
                        eng.wait_ge(max_done, b * MAXIMA + MAXIMA)
                        wait_free(eng, step, b)
                        for t in range(NT):
                            mm = eng.transpose(bank(step)[0:H, 0, t * P:(t + 1) * P], nmx[:, t, :], ident[:, :])
                        mm.then_inc(done(step), 1)
                    elif kind == "SROW":
                        wait_read(eng, ("SMAX", NG - 1, 2 * NT - 2), b)
                        wait_read(eng, ("SMAX", NG - 1, 2 * NT - 1), b)
                        wait_free(eng, step, b)
                        for t in range(NT):
                            mm = eng.transpose(bank(step)[0:H, 0, t * P:(t + 1) * P], esum[:, t, :], ident[:, :])
                        mm.then_inc(done(step), 1)
                    elif kind == "X2T":
                        t = step[1]
                        wait_read(eng, ("PV1", t), i)
                        wait_free(eng, step, i)
                        transpose4(step, x1[:, t, :], done(step))
                    elif kind == "HID":
                        t = step[1]
                        if t == 0:
                            eng.wait_ge(par_in, i * 96 + 96)
                        wait_free(eng, step, i)
                        for d in range(ND):
                            mm = eng.matmul(lone[2][:, 0:P], w1[:, d, :], x2T[:, t % 2, d * P:(d + 1) * P],
                                            start=(d == 0), stop=(d == ND - 1))
                        mm.then_inc(done(step), 1)
                    elif kind == "ADP":
                        wait_free(eng, step, i)
                        eng.matmul(lone[2][:, :], hT[:, step[1] % 2, :], w2[:, :], start=True, stop=True
                                   ).then_inc(done(step), 1)
                    elif kind == "X3T":
                        t = step[1]
                        eng.wait_ge(x3_done, i * NT + t + 1)
                        wait_free(eng, step, i)
                        transpose4(step, x1[:, t, :], done(step))
                    elif kind == "LOW":
                        t = step[1]
                        wait_free(eng, step, i)
                        for d in range(ND):
                            mm = eng.matmul(lone[2][0:RANK, 0:P], ecol[:, 4 + d * RANK:4 + (d + 1) * RANK],
                                            x3T[:, t % 2, d * P:(d + 1) * P], start=(d == 0), stop=(d == ND - 1))
                        mm.then_inc(done(step), 1)
                    elif kind == "LORA":
                        if step[1] == 0:
                            eng.wait_ge(emb_in, i * 16 + 16)
                        wait_free(eng, step, i)
                        eng.matmul(lone[2][:, :], lowT[:, step[1] % 2, :], lowB[:, :], start=True, stop=True
                                   ).then_inc(done(step), 1)

            def scores(n, i):
                g, k = divmod(n, NT)
                for u in range(2):
                    step = ("ST", g, k, u)
                    wait_free(eng, step, i)
                    for j in (2 * u, 2 * u + 1):
                        mm = eng.matmul(bank(step)[:, j % 2, :], KQ[0:SHIFT_ROW + 1, j, g, 0, k * P:(k + 1) * P],
                                        KQ[0:SHIFT_ROW + 1, j, g, 1, :], start=True, stop=True)
                    mm.then_inc(done(step), 1)

            def values(n, i):
                g, k = divmod(n, NT)
                if k == 0:
                    wait_free(eng, ("PV", g), i)
                if g == 0:
                    wait_read(eng, ("V", k), i)
                for u in range(2):
                    wait_read(eng, ("ST", g, k, u), i)
                for j in range(NJ):
                    q = slice(j * DH, (j + 1) * DH)
                    mm = eng.matmul(bank(("PV", g))[q, :], V[:, k, g * P + j * DH:g * P + (j + 1) * DH],
                                    big[:, n % 2, j, :], start=(k == 0), stop=(k == NT - 1), skip_group_check=True)
                mm.then_inc(pv_done if k < NT - 1 else done(("PV", g)), 1)

            def spread_norms(g, i):
                if g == 0:
                    eng.wait_ge(norms_lo, i + 1)
                for n, name in enumerate(("NORMS", "SELFW")):
                    wait_free(eng, (name, g), i)
                    eng.matmul(lone[2 + n][:, :], head_rows[:, g, :], norms16[:, n, :], start=True, stop=True
                               ).then_inc(done((name, g)), 1)

            def small_tables(i):
                eng.wait_ge(prep_in, i * 48 + 48)
                wait_free(eng, ("PREPA",), i)
                wait_free(eng, ("PREPB",), i)
                for d in range(ND):
                    mm = eng.transpose(lone[2][0:RANK, d * P:(d + 1) * P], smallb[:, d, :], ident[:, :])
                mm.then_inc(done(("PREPB",)), 1)
                eng.transpose(lone[3][:, 0:4], erow[:, :], ident[0:NT, 0:NT])
                for d in range(ND):
                    mm = eng.transpose(lone[3][:, 4 + d * RANK:4 + (d + 1) * RANK],
                                       small[:, d * P:(d + 1) * P], ident[0:RANK, 0:RANK])
                mm.then_inc(done(("PREPA",)), 1)

            def attention(i):
                eng.wait_ge(shift_in, i * 16 + 16)
                scores(0, i)
                for n in range(NSTEP):
                    if n + 1 < NSTEP:
                        scores(n + 1, i)
                    values(n, i)
                    if NT <= n < NT + NG:
                        spread_norms(n - NT, i)
                    if n == NSTEP - 3:
                        small_tables(i)

            def next_x(step, i):
                n = step[1]
                eng.wait_ge(tile_in[n], i * 32 + 48)
                wait_free(eng, step, i)
                transpose4(step, tiles_in[:, n, :], done(step))

            def layer1(i, head):
                for step in ORDER_L1:
                    kind, t = step[0], step[-1]
                    if kind == "NIN" and head:
                        next_x(step, i)
                    elif kind == "WOP":
                        at = slice(t * P, (t + 1) * P)
                        if t == 0:
                            eng.wait_ge(att_lo, i * NG + NG - 1)
                        wait_free(eng, ("WO", t - t % 2), i)
                        hi_lo(eng, bank(("WO", t))[:, t % 2, :],
                              [(aT[:, 0, g, at], aT[:, 1, g, at]) for g in range(NG - 1)],
                              [(w_hi[:, 3, g, :], w_lo[:, 3, g, :]) for g in range(NG - 1)], last=False)
                    elif kind == "WO":
                        g, at = NG - 1, slice(t * P, (t + 1) * P)
                        if t == 0:
                            eng.wait_ge(att_lo, i * NG + NG)
                        hi_lo(eng, bank(step)[:, t % 2, :], [(aT[:, 0, g, at], aT[:, 1, g, at])],
                              [(w_hi[:, 3, g, :], w_lo[:, 3, g, :])], first=False).then_inc(done(step), 1)
                    elif kind == "X1T":
                        eng.wait_ge(q1_done, i * NT + t + 1)
                        wait_free(eng, step, i)
                        transpose4(step, q1[:, t % 2, :], done(step))
                    elif kind == "S1":
                        wait_read(eng, ("X1T", t), i)
                        wait_free(eng, step, i)
                        hi_lo(eng, bank(step)[:, :],
                              [(q1T[:, t % 2, 0, d, :], q1T[:, t % 2, 1, d, :]) for d in range(ND)],
                              [(fT[:, 0, d, :], fT[:, 1, d, :]) for d in range(ND)]).then_inc(done(step), 1)
                    elif kind == "P1T":
                        wait_read(eng, ("S1", t), i)
                        wait_free(eng, step, i)
                        transpose4(step, p1[:, t % 2, :], done(step))
                    elif kind == "PV1":
                        if t == 0:
                            eng.wait_ge(f_lo, i * NT + NT)
                        wait_read(eng, ("P1T", t), i)
                        wait_free(eng, step, i)
                        hi_lo(eng, bank(step)[:, 0, :],
                              [(p1T[:, t % 2, 0, k, :], p1T[:, t % 2, 1, k, :]) for k in range(NT)],
                              [(f16[:, 0, k, :], f16[:, 1, k, :]) for k in range(NT)]).then_inc(done(step), 1)

            eng.wait_ge(free[2], 1)
            vector_rows(0)
            for n in range(NT):
                next_x(("NIN", n), -1)
            vector_rows(1)
            vector_cols(0)
            vector_cols(1)
            eng.wait_ge(w_lo_done, 2)
            mid(False, True, 0)
            with eng.Fori(0, B - 1) as i:
                attention(i)
                layer1(i, True)
                mid(True, True, i)
            attention(B - 1)
            layer1(B - 1, False)
            mid(True, False, B - 1)


_INS = ['x', 'fside_BxSxS_0', 'itok_B_18_1004', 'itok_B_0_5', 'itok_B_0_8', 'itok_B_0_3',
        'L0_cond_Wq', 'L0_cond_bq', 'L0_cond_Wk', 'L0_cond_bk', 'L0_cond_Wv', 'L0_cond_bv', 'L0_cond_Wo',
        'L0_cond_bo', 'L0_cond_b_prev', 'L0_cond_b_self', 'L1_cond_braak_embed', 'L2_cond_W1', 'L2_cond_b1',
        'L2_cond_W2', 'L2_cond_b2', 'L2_cond_gamma', 'L2_cond_beta', 'L3_cond_lora_A', 'L3_cond_lora_B',
        'L3_cond_lang_embed']
_OUTS = [((B, S, D), 'float32')]


def kernel(**inputs):
    import numpy as _np
    import concourse.bacc as _bacc
    from concourse import mybir as _mybir
    from concourse.bass_utils import run_bass_kernel_spmd as _run

    nc = _bacc.Bacc("TRN2", target_bir_lowering=False, num_devices=1)
    arrays, args = {}, []
    for name in _INS:
        a = _np.ascontiguousarray(inputs[name])
        arrays[f"in_{name}_dram"] = a
        args.append(nc.dram_tensor(f"in_{name}_dram", a.shape, _mybir.dt.from_np(a.dtype), kind="ExternalInput").ap())
    for n, (shape, dtype) in enumerate(_OUTS):
        dt = _mybir.dt.from_np(_np.dtype(dtype))
        args.append(nc.dram_tensor(f"out_{n}_dram", shape, dt, kind="ExternalOutput").ap())
    build_program(nc, *args)
    r = _run(nc, [arrays], core_ids=[0])
    got = tuple(r.results[0][f"out_{n}_dram"] for n in range(len(_OUTS)))
    return got[0]
```

```python
from contextlib import ExitStack

import concourse.bass as bass
from concourse import mybir

F32 = mybir.dt.float32
F16 = mybir.dt.float16
I32 = mybir.dt.int32
ALU = mybir.AluOpType
ACT = mybir.ActivationFunctionType
AX_X = mybir.AxisListType.X

B, S, D = 8, 512, 512
H, DH = 16, 32
P = 128
NT = S // P
ND = D // P
NG, NJ = H // 4, 4
NSTEP = NG * NT
STAGES, LANGS, A, RLANGS, RANK = 6, 10, 128, 4, 16
SCALE = 1.0 / float(DH) ** 0.5
EPS = 1e-5
WS = 64.0
BIG = 32768.0
RS = 1024.0
PS = 1024.0
MASK_ROW = 3 * DH
SHIFT_ROW = MASK_ROW + 1
DMAS_PER_STACK = 3 * NJ * 16
LOW_ROW = 32
LR = 32
NROWS = LOW_ROW + H



def order_mid(tail, head):
    adapters = []
    if tail:
        n0, n2 = ([("NORM", t, n) for n in range(NORM_PIECES)] for t in (0, 2))
        adapters = [("X2T", 0), None, ("HID", 0), None, ("ADP", 0), None, ("X2T", 1), ("SQ", 0), ("HID", 1), ("ADP", 1),
                    ("SQ", 1), n0[0], ("X2T", 2), n0[1], ("HID", 2), n0[2], ("X2T", 3), n0[3], ("HID", 3), n0[4],
                    n0[5], None, ("SCALE", 0), None, ("SCALE", 1), ("X3T", 0), None, ("LOW", 0), None, ("ADP", 2),
                    None, ("ADP", 3), ("SQ", 2), ("LORA", 0), ("SQ", 3), ("X3T", 1), n2[0], ("LOW", 1), n2[1],
                    n2[2], ("LORA", 1), n2[3], n2[4], n2[5], ("SCALE", 2), None, ("SCALE", 3), ("X3T", 2), None,
                    ("LOW", 2), None, ("LORA", 2), ("X3T", 3), None, ("LOW", 3), None, ("LORA", 3)]
    if not head:
        return [step for step in adapters if step]


    def parts(step):
        return [("PART", n, step) for n in range(PARTS - 1)] + [step]

    slots = [("IN", NT), ("IN", NT + 1), ("PART", 0, ("K", 0)), ("IN", NT + 2), ("PART", 1, ("K", 0)),
             ("IN", NT + 3), ("K", 0)] + parts(("Q", 0)) + parts(("KS", 0))
    for g in range(1, NG):
        slots += parts(("K", g)) + parts(("Q", g)) + parts(("KS", g))
    for kind in ("VS", "V"):
        for n in range(NG):
            slots += parts((kind, n))
    opens = [slots.index(("Q", g)) + OPEN[g] for g in range(NG)]
    maxima = [("SMAX", g, u) for g in range(NG) for u in range(2 * NT)]
    out, later = [], {}
    f16_at = slots.index(("KS", NG - 1)) + F16_AFTER
    for n in range(NT):
        later[f16_at + 2 * n] = [("F16", n)]
    rows = sums = False
    for i, step in enumerate(slots):
        out.append(step)
        out += later.get(i, [])
        if maxima and i >= opens[maxima[0][1]]:
            out.append(maxima.pop(0))
        elif not maxima and not rows:
            out.append(("MROW",))
            rows = True
            late = i + PARTS
        if adapters:
            out += [a for a in (adapters.pop(0),) if a]
        if rows and not sums and i >= late and not adapters:
            out.append(("SROW",))
            sums = True
        if step[0] in ("K", "Q"):
            later.setdefault(i + 1, []).append(("HALF",) + step)
        if step[0] == "KS":
            later.setdefault(i + 2 * PARTS, []).append(("SELF", step[1]))
        if step == ("VS", 2):
            later.setdefault(i + PARTS - 1, []).append(("NEG",))
    assert rows and i >= max(later)
    return out + [a for a in adapters if a] + ([] if sums else [("SROW",)])


OPEN = (16, 13, 13, 13)
F16_AFTER = 6
PARTS = 3
NORMS_AT = (5, 7, 8, 9)
NEWTON = 15
NORM_PIECES = 6

ORDER_L1 = [("WOP", 1), ("WOP", 2), ("WO", 0), ("WO", 1), ("WOP", 3), ("X1T", 0), ("X1T", 1), ("WO", 2),
            ("WO", 3), ("S1", 0), ("X1T", 2), ("S1", 1), ("X1T", 3), ("P1T", 0), ("S1", 2),
            ("P1T", 1), ("PV1", 0), ("S1", 3), ("P1T", 2), ("PV1", 1), ("NIN", 0), ("P1T", 3), ("NIN", 1),
            ("PV1", 2), ("NIN", 2), ("NIN", 3), ("PV1", 3)]


NIN_BANKS = (3, 0, 3, 1)


def plan_banks():
    uses = {k: [] for k in (0, 1, 2, 3, 4, 6)}

    def give(bank, step):
        uses[bank].append(step)

    n = m = 0
    for step in order_mid(False, True):
        if step[0] == "IN":
            give((1, 3)[step[1] % 2], step)
        elif step[0] in ("Q", "K", "KS", "VS", "V"):
            give(n % 2, step)
            n += 1
        elif step[0] == "SMAX":
            give((4, 6)[m % 2], step)
            m += 1
        elif step[0] in ("MROW", "SROW"):
            give({"MROW": 4, "SROW": 6}[step[0]], step)
    for g in range(NG):
        give(3, ("SELF", g))
    for g in range(NG):
        give(2, ("NORMS", g))
        give(3, ("SELFW", g))
        give(g % 2, ("PV", g))
        for k in range(NT):
            give(4, ("ST", g, k, 0))
            give(6, ("ST", g, k, 1))
    give(2, ("PREPB",))
    give(3, ("PREPA",))
    ring = {"X1T": (0, 1), "P1T": (0, 1), "S1": (2, 3), "PV1": (4, 6), "NIN": NIN_BANKS}
    for t in range(NT):
        give((4, 6)[t // 2], ("WO", t))
    for step in ORDER_L1:
        if step[0] in ring:
            give(ring[step[0]][step[1] % len(ring[step[0]])], step)
    for step in order_mid(True, False):
        if step[0] not in ("NORM", "SCALE", "SQ"):
            give(2, step)
    where = {step: (k, c) for k, steps in uses.items() for c, step in enumerate(steps)}
    return where, {k: len(steps) for k, steps in uses.items()}


WHERE, USES = plan_banks()
ADAPTER_BANKS = (2, 3, 0, 1)


def order_last():
    norm = {t: [("NORM", t, n) for n in range(NORM_PIECES)] for t in (0, 2)}
    cut = ORDER_L1.index(("PV1", 1)) + 1
    return ([step for step in ORDER_L1[:cut]]
            + [("X2T", 0), ("P1T", 3), ("HID", 0), ("X2T", 1), ("PV1", 2), ("ADP", 0), ("HID", 1), ("SQ", 0),
               ("PV1", 3), ("ADP", 1), ("SQ", 1), ("X2T", 2)] + norm[0]
            + [("HID", 2), ("X2T", 3), ("SCALE", 0), ("HID", 3), ("X3T", 0), ("SCALE", 1), ("ADP", 2), ("LOW", 0),
               ("X3T", 1), ("SQ", 2), ("ADP", 3), ("LOW", 1), ("SQ", 3)] + norm[2]
            + [("LORA", 0), ("LORA", 1), ("SCALE", 2), ("X3T", 2), ("SCALE", 3), ("LOW", 2), ("X3T", 3),
               ("LORA", 2), ("LOW", 3), ("LORA", 3)])


def plan_last():
    order = [step for step in order_last() if step in WHERE and step[0] != "WO"]
    skip = [step for step in WHERE if step in order or step[0] == "NIN"]
    count = {k: (B - 1) * USES[k] + BEFORE[k] + min([WHERE[step][1] for step in skip if WHERE[step][0] == k]
                                                  + [USES[k]]) for k in USES}
    where = {}
    for step in order:
        k = ADAPTER_BANKS[step[1]] if step in ADAPTER_STEPS else WHERE[step][0]
        where[step] = (k, count[k])
        count[k] += 1
    return where


ADAPTER_STEPS = set(order_mid(True, False))
BEFORE = {k: NIN_BANKS.count(k) + (k == 2) for k in USES}
LAST = plan_last()


def build_program(nc, x, f, len_, stage_, lang_, rlang_, Wq, bq, Wk, bk, Wv, bv, Wo, bo, b_prev, b_self,
                  embed, W1, b1, W2, b2, gamma, beta, lora_A, lora_B, lang_embed, out):
    ctx = ExitStack()
    with ctx:
        def sb(name, shape, dt=F32):
            return ctx.enter_context(nc.sbuf_tensor(name, shape, dt))

        def sem(name):
            return ctx.enter_context(nc.semaphore(name))

        ident = sb("ident", [P, P])
        w_hi = sb("w_hi", [P, 4, ND, D], F16)
        w_lo = sb("w_lo", [P, 4, ND, D], F16)
        ones = sb("ones", [P, 1])
        vecs = sb("vecs", [20, P])
        cols = sb("cols", [P, 20])
        bias_q = sb("bias_q", [P, NG])
        bias_k = sb("bias_k", [P, NG])
        bias_ks = sb("bias_ks", [P, NG])
        bo_rows = sb("bo_rows", [P, D])
        head_cols = sb("head_cols", [P, NG, H])
        head_rows = sb("head_rows", [NROWS, NG, P], F16)
        tiles_in = sb("tiles_in", [P, NT, D])
        xT = sb("xT", [P, 2, ND, S], F16)
        fT = sb("fT", [P, 2, ND, S], F16)
        f16 = sb("f16", [P, 2, NT, D], F16)
        qk32 = sb("qk32", [P, 3, S])
        half = sb("half", [P, 2, 4, S], F16)
        prod = sb("prod", [P, S])
        KQ = sb("KQ", [P, NJ, NG, 2, S], F16)
        V = sb("V", [P, NT, D])
        vsT = sb("vsT", [P, NG, S])
        nmx = sb("nmx", [P, NT, H])
        esum = sb("esum", [P, NT, H])
        self2 = sb("self2", [H, 2, S])
        norms16 = sb("norms16", [NROWS, 2, S], F16)
        shift = sb("shift", [H, S], F16)
        big = sb("big", [P, 2, NJ, S])
        t1 = sb("t1", [P, S])
        t2 = sb("t2", [P, S])
        x1 = sb("x1", [P, NT, D])
        ecol = sb("ecol", [P, NT + ND * LR])
        q1 = sb("q1", [P, 2, D])
        q1T = sb("q1T", [P, 2, 2, ND, P], F16)
        p1_both = sb("p1_both", [P, 2, 2, S])
        nmax = sb("nmax", [P, 2])
        rsum = sb("rsum", [P, 2])
        rrec = sb("rrec", [P, NT])
        hT = sb("hT", [P, 2, P])
        y = sb("y", [P, 2, D])
        st = sb("st", [P, 2, 8])
        lowT = sb("lowT", [P, 2, P])
        w1 = sb("w1", [P, ND, A])
        w2 = sb("w2", [P, D])
        b1c = sb("b1c", [P, 1])
        b2r = sb("b2r", [P, D])
        gr = sb("gr", [P, D])
        br = sb("br", [P, D])
        small = sb("small", [LR, D])
        smallb = sb("smallb", [P, ND, RANK])
        smallb4 = sb("smallb4", [P, ND, ND, LR])
        erow = sb("erow", [NT, P])
        lowB = sb("lowB", [P, D])
        idx = sb("idx", [1, 4 * B], I32)
        lens_i = sb("lens_i", [B, 1], I32)
        lens_f = sb("lens_f", [B, 1])
        aT = xT
        p1 = p1_both[:, 0]
        p1T = p1_both[:, 1].bitcast(F16).rearrange("p a (h k n) -> p a h k n", h=2, k=NT)
        spread = p1_both[:].rearrange("p a b n -> p (a b) n")
        norms = q1[0:H]
        head_rows32 = t2[0:NROWS, :].rearrange("p (g n) -> p g n", g=NG)
        W_ORDER = (1, 0, 2, 3)
        x2T, xb, x3T, junk = big[:, 0, 0:2], big[:, 0, 2:4], big[:, 1, 0:2], big[:, 1, 2:4]
        stage32 = [big[:, n].rearrange("p a n -> p (a n)") for n in range(2)]
        stage32 = [s_.rearrange("p (a n) -> p a n", a=ND) for s_ in stage32]
        kpos = t1[0:B, :]
        mask16 = half[0:B, 0, 0, :]
        mask_dram = nc.dram_tensor("mask_rows", (B, S), F16, kind="Internal").ap()

        lone = {k: ctx.enter_context(nc.psum_tensor(f"bank{k}", [P, 512], F32)) for k in range(4)}
        pair = {k: ctx.enter_context(nc.psum_tensor(f"banks{k}", [P, 2, 512], F32)) for k in (4, 6)}
        full = {k: sem(f"full{k}") for k in USES}
        free = {k: sem(f"free{k}") for k in USES}

        def place(step, b):
            if isinstance(b, int) and b == B - 1 and step in LAST:
                return LAST[step]
            k, c = WHERE[step]
            return k, b * USES[k] + (BEFORE[k] + c)

        def bank(step, b=0):
            k = place(step, b)[0]
            return lone[k] if k < 4 else pair[k]

        def tile_of(step, b):
            view = bank(step, b)
            return view[:, 0, :] if len(view.shape) == 3 else view[:, :]

        def wait_free(eng, step, b):
            k, c = place(step, b)
            eng.wait_ge(free[k], c)

        def wait_full(eng, step, b):
            k, c = place(step, b)
            eng.wait_ge(full[k], c + 1)

        def wait_read(eng, step, b):
            k, c = place(step, b)
            eng.wait_ge(free[k], c + 1)

        def done(step, b=0):
            return full[place(step, b)[0]]

        def read(step, b=0):
            return free[place(step, b)[0]]

        vec_in = sem("vec_in")
        bo_in = sem("bo_in")
        idx_in = sem("idx_in")
        len_in = sem("len_in")
        w_in = [sem("w_in0"), sem("w_in1")]
        consts = sem("consts")
        sel_ready = sem("sel_ready")
        rows_ready = sem("rows_ready")
        stack_rows = sem("stack_rows")
        w_hi_done = sem("w_hi_done")
        w_lo_done = sem("w_lo_done")
        bias_row = sem("bias_row")
        sums_done = sem("sums_done")
        bias_full = sem("bias_full")
        bias_done = sem("bias_done")
        len_cast = sem("len_cast")
        mask_made = sem("mask_made")
        mask_out = sem("mask_out")
        tile_in = [sem(f"tile_in{n}") for n in range(NT)]
        in_hi = sem("in_hi")
        f_hi = sem("f_hi")
        f_lo = sem("f_lo")
        qk_hi = sem("qk_hi")
        qk_lo = sem("qk_lo")
        stacked = [sem(f"stacked{g}") for g in range(NG)]
        mask_in = sem("mask_in")
        shift_in = sem("shift_in")
        max_done = sem("max_done")
        MAXIMA = H * NT
        self_neg = sem("self_neg")
        self_diff = sem("self_diff")
        self_exp = sem("self_exp")
        den = sem("den")
        norms_done = sem("norms_done")
        norms_hi = sem("norms_hi")
        norms_lo = sem("norms_lo")
        pv_done = sem("pv_done")
        att_f32 = sem("att_f32")
        att_hi = sem("att_hi")
        att_lo = sem("att_lo")
        x_in = sem("x_in")
        prep_in = sem("prep_in")
        copied = sem("copied")
        emb_in = sem("emb_in")
        par_in = sem("par_in")
        x_bo = sem("x_bo")
        q1_done = sem("q1_done")
        q1_hi = sem("q1_hi")
        max1 = sem("max1")
        sum1 = sem("sum1")
        rec1 = sem("rec1")
        p1_hi = sem("p1_hi")
        xb_done = sem("xb_done")
        xg_done = sem("xg_done")
        mean_done = sem("mean_done")
        sq_done = sem("sq_done")
        newton = sem("newton")
        normed = sem("normed")
        scaled = sem("scaled")
        x3_done = sem("x3_done")
        stored = sem("stored")

        def wait_used(eng, n, i):
            g, k = divmod(n, NT)
            if k == NT - 1:
                wait_full(eng, ("PV", g), i)
            else:
                eng.wait_ge(pv_done, i * NG * (NT - 1) + g * (NT - 1) + k + 1)

        in_loop = nc.Block()
        block = ctx.enter_context(in_loop)

        def hi_lo(eng, out_ap, left, right, first=True, last=True, part=None):
            pairs = [(l[lh], r[rh]) for l, r in zip(left, right) for lh, rh in ((0, 0), (1, 0), (0, 1))]
            each = len(pairs) // PARTS
            at = range(len(pairs)) if part is None else range(part * each, (part + 1) * each)
            for n in at:
                mm = eng.matmul(out_ap, pairs[n][0], pairs[n][1], start=(first and n == 0),
                                stop=(last and n == len(pairs) - 1))
            return mm

        @block.gpsimd
        def _(eng):
            eng.memset(ident[:, :], 0.0).then_inc(consts, 1)
            eng.memset(head_cols[:, :, :], 0.0).then_inc(consts, 1)
            eng.memset(head_rows32[:, :, :], 0.0).then_inc(consts, 1)
            eng.wait_ge(consts, 3)
            eng.memset(ones[:, :], 1.0).then_inc(consts, 1)
            eng.wait_ge(consts, 4)
            eng.affine_select(out=ident[:, :], in_=ident[:, :], compare_op=ALU.not_equal, fill=1.0,
                              base=0, pattern=[[-1, P]], channel_multiplier=1).then_inc(sel_ready, 1)
            for n, low in enumerate((0, LOW_ROW)):
                for g in range(NG):
                    v = head_rows32[:, g, :].rearrange("h (j d) -> h j d", j=NJ)
                    eng.wait_ge(sel_ready, 1 + NG * n + g)
                    eng.affine_select(out=v, in_=v, compare_op=ALU.not_equal, fill=1.0 / RS, base=-g - low,
                                      pattern=[[-NG, NJ], [0, DH]], channel_multiplier=1).then_inc(sel_ready, 1)
            eng.wait_ge(sel_ready, 1 + 2 * NG)
            eng.iota(kpos, pattern=[[1, S]], base=0, channel_multiplier=0,
                     allow_small_or_imprecise_dtypes=True).then_inc(sel_ready, 1)
            eng.wait_ge(sel_ready, 2 + 2 * NG)
            eng.memset(KQ[MASK_ROW:P, :, :, 1, :], BIG).then_inc(stack_rows, 1)
            eng.wait_ge(stack_rows, 1)
            eng.memset(KQ[MASK_ROW:P, :, :, 0, :], 1.0).then_inc(stack_rows, 1)
            eng.wait_ge(stack_rows, 2)

            def split(high, low, src, high_done, count, low_done):
                eng.tensor_tensor(high, src, ones[:, 0:1].to_broadcast([P, S]), ALU.mult).then_inc(high_done, 1)
                eng.wait_ge(high_done, count)
                eng.tensor_tensor(low, src, high, ALU.subtract).then_inc(low_done, 1)

            def mid(tail, head, i, order=None):
                b = i + 1 if tail else i
                for step in order or order_mid(tail, head):
                    if step[0] == "F16":
                        n = step[1]
                        wait_full(eng, ("IN", NT + n), b)
                        if tail:
                            wait_full(eng, ("PV1", NT - 1), i)
                        split(f16[:, 0, n, :], f16[:, 1, n, :], tiles_in[:, n, :], f_hi, b * NT + n + 1, f_lo)
                    elif step[0] == "HALF":
                        g, k = step[2], int(step[1] == "K")
                        wait_read(eng, step[1:], b)
                        if g >= 2:
                            eng.wait_ge(stacked[g - 2], b * DMAS_PER_STACK + DMAS_PER_STACK)
                        elif tail:
                            eng.wait_ge(stacked[NG - 2 + g], i * DMAS_PER_STACK + DMAS_PER_STACK)
                        hi = 0 if k else 2
                        split(half[:, g % 2, hi, :], half[:, g % 2, hi + 1, :], qk32[:, 2 if k else g % 2, :],
                              qk_hi, b * 2 * NG + 2 * g + 2 - k, qk_lo)
                    elif step[0] == "X2T":
                        t = step[1]
                        if t >= 2:
                            wait_read(eng, ("ADP", t - 2), i)
                        else:
                            wait_used(eng, NSTEP - 1, i)
                        if t == 0:
                            eng.wait_ge(par_in, i * 96 + 96)
                        wait_read(eng, ("PV1", t), i)
                        eng.tensor_tensor(xb[:, t % 2, :], x1[:, t, :], b2r[:, :], ALU.add).then_inc(xb_done, 1)
                    elif step[0] == "NORM" and step[2] == 0:
                        for t in (step[1], step[1] + 1):
                            wait_full(eng, ("X2T", t), i)
                            eng.wait_ge(xb_done, i * NT + t + 1)
                            eng.tensor_tensor(x1[:, t, :], x1[:, t, :], br[:, :], ALU.add).then_inc(xg_done, 1)
                    elif step[0] == "SCALE":
                        t = step[1]
                        eng.wait_ge(normed, i * NT + t + 1)
                        eng.tensor_tensor(y[:, t % 2, :], y[:, t % 2, :], gr[:, :], ALU.mult).then_inc(scaled, 1)
                        eng.wait_ge(scaled, i * NT + t + 1)
                        eng.wait_ge(xg_done, i * NT + t + 1)
                        eng.tensor_tensor(x1[:, t, :], y[:, t % 2, :], x1[:, t, :], ALU.add).then_inc(x3_done, 1)

            def add_bo(i):
                eng.wait_ge(x_in, i * 16 + 16)
                for t in range(NT):
                    eng.tensor_tensor(x1[:, t, :], x1[:, t, :], bo_rows[:, :], ALU.add).then_inc(x_bo, 1)

            eng.wait_ge(bo_in, 16)
            eng.wait_ge(mask_out, 16)
            mid(False, True, 0)
            with eng.Fori(0, B - 1) as i:
                add_bo(i)
                mid(True, True, i)
            add_bo(B - 1)
            mid(True, False, B - 1, [step for step in order_last() if step in ADAPTER_STEPS])

        @block.sync
        def _(eng):
            def load_weight(n):
                w = (Wk, Wq, Wv, Wo)[n]
                eng.dma_start(stage32[n % 2], w.rearrange("(t p) n -> p t n", p=P)).then_inc(w_in[n % 2], 16)

            def load_tile(n, b):
                src = x if n < NT else f
                t = n % NT
                if isinstance(b, int):
                    rows = src[b, t * P:(t + 1) * P, :]
                else:
                    rows = src[bass.ds(b, 1), t * P:(t + 1) * P, :].rearrange("a p n -> (a p) n")
                eng.dma_start(tiles_in[:, t, :], rows).then_inc(tile_in[t], 16)

            def whole(src, b):
                if isinstance(b, int):
                    return src[b].rearrange("(t p) n -> p t n", p=P)
                return src[bass.ds(b, 1), :, :].rearrange("a (t p) n -> p (a t) n", p=P)

            def mid(tail, head, i, order=None):
                b = i + 1 if tail else i
                for step in order or order_mid(tail, head):
                    if step[0] == "HALF":
                        g, k = step[2], int(step[1] == "K")
                        if g == 0 and k:
                            row = mask_dram[bass.ds(b, 1), :] if tail else mask_dram[b:b + 1, :]
                            if tail:
                                wait_full(eng, ("ST", NG - 1, NT - 1, 1), i)
                            else:
                                eng.wait_ge(stack_rows, 2)
                            eng.dma_start(KQ[MASK_ROW:MASK_ROW + 1, :, :, 0, :].rearrange("o j g n -> o (j g) n"),
                                          row.to_broadcast([H, S]).rearrange("(o h) n -> o h n", o=1)
                                          ).then_inc(mask_in, 16)
                        if not k:
                            eng.wait_ge(qk_lo, b * 2 * NG + 2 * g + 2)
                            for r, parts in enumerate((slice(0, 3, 2), slice(1, 3), slice(0, 4, 3))):
                                for j in range(NJ):
                                    eng.dma_start(KQ[r * DH:(r + 1) * DH, j, g, :, :],
                                                  half[j * DH:(j + 1) * DH, g % 2, parts, :]
                                                  ).then_inc(stacked[g], 16)
                    elif step[0] == "MROW":
                        wait_read(eng, step, b)
                        eng.dma_start(KQ[SHIFT_ROW:SHIFT_ROW + 1, :, :, 1, :].rearrange("o j g n -> o (j g) n"),
                                      shift[:, :]).then_inc(shift_in, 16)
                    elif step[0] == "LORA":
                        t = step[1]
                        wait_read(eng, step, i)
                        if isinstance(i, int):
                            dst = out[i, t * P:(t + 1) * P, :]
                        else:
                            dst = out[bass.ds(i, 1), t * P:(t + 1) * P, :].rearrange("a p n -> (a p) n")
                        eng.dma_start(dst, x1[:, t, :]).then_inc(stored, 16)

            def params(i):
                stage = eng.value_load(idx[0:1, bass.ds(i, 1)], min_val=0, max_val=STAGES - 1)
                lang = eng.value_load(idx[0:1, bass.ds(i + B, 1)], min_val=0, max_val=LANGS - 1)
                rlang = eng.value_load(idx[0:1, bass.ds(i + 2 * B, 1)], min_val=0, max_val=RLANGS - 1)
                eng.wait_ge(norms_done, i + 1)
                eng.dma_start(x1[:, :, :], whole(x, i)).then_inc(x_in, 16)
                eng.dma_start(erow[:, :], embed[bass.ds(stage, 1), :].rearrange("a (t p) -> (a t) p", p=P)
                              ).then_inc(prep_in, 16)
                eng.dma_start(small[0:RANK, :], lora_A[bass.ds(rlang, 1), :, :].rearrange("a r n -> (a r) n")
                              ).then_inc(prep_in, 16)
                eng.dma_start(smallb[:, :, :], lora_B[bass.ds(rlang, 1), :, :].rearrange("a (t p) r -> p (a t) r", p=P)
                              ).then_inc(prep_in, 16)
                eng.dma_start(w1[:, :, :], W1[bass.ds(lang, 1), :, :].rearrange("a (t p) n -> p (a t) n", p=P)
                              ).then_inc(par_in, 16)
                eng.dma_start(w2[:, :], W2[bass.ds(lang, 1), :, :].rearrange("a p n -> (a p) n")).then_inc(par_in, 16)
                eng.dma_start(b1c[:, :], b1[bass.ds(lang, 1), :].rearrange("a (p o) -> (a p) o", o=1)
                              ).then_inc(par_in, 16)
                for dst, src in ((b2r, b2), (gr, gamma), (br, beta)):
                    eng.dma_start(dst[:, :], src[bass.ds(lang, 1), :].to_broadcast([P, D])).then_inc(par_in, 16)

            def language_row(i):
                rlang = eng.value_load(idx[0:1, bass.ds(i + 2 * B, 1)], min_val=0, max_val=RLANGS - 1)
                wait_read(eng, ("PREPB",), i)
                eng.dma_start(lowB[RANK:RANK + 1, :], lang_embed[bass.ds(rlang, 1), :]).then_inc(emb_in, 16)

            def swap_tiles(i):
                for n in range(NT):
                    wait_full(eng, ("NIN", n), i)
                    load_tile(n + NT, i + 1)

            def prefetch(i):
                for t in range(NT):
                    eng.wait_ge(f_lo, i * NT + t + 1)
                    load_tile(t, i + 1)

            load_weight(0)
            for n, v in enumerate((bq, bk, bv, b_self, b_prev)):
                flat = v if len(v.shape) == 1 else v.rearrange("a c n -> (a c n)")
                eng.dma_start(vecs[4 * n:4 * n + 4, :], flat.rearrange("(t p) -> t p", p=P)).then_inc(vec_in, 16)
            eng.dma_start(lens_i[:, :], len_.rearrange("(n a) -> n a", a=1)).then_inc(len_in, 16)
            for t in range(NT):
                load_tile(t, 0)
            load_weight(1)
            for n, v in enumerate((stage_, lang_, rlang_)):
                eng.dma_start(idx[:, n * B:(n + 1) * B], v.rearrange("(a n) -> a n", a=1)).then_inc(idx_in, 16)
            eng.dma_start(bo_rows[:, :], bo.rearrange("(a n) -> a n", a=1).to_broadcast([P, D])).then_inc(bo_in, 16)
            swap_tiles(-1)
            eng.wait_ge(mask_made, 1)
            eng.dma_start(mask_dram, mask16).then_inc(mask_out, 16)
            for n in (2, 3):
                eng.wait_ge(w_lo_done, n - 1)
                eng.wait_ge(bias_full, 2)
                load_weight(n)
            eng.wait_ge(mask_out, 16)
            eng.wait_ge(idx_in, 48)
            mid(False, True, 0)
            with eng.Fori(0, B - 1) as i:
                params(i)
                prefetch(i)
                language_row(i)
                swap_tiles(i)
                mid(True, True, i)
            params(B - 1)
            language_row(B - 1)
            mid(True, False, B - 1, [step for step in order_last() if step in ADAPTER_STEPS])
            eng.wait_ge(stored, B * NT * 16)

        @block.scalar
        def _(eng):
            def weight_high(n):
                eng.wait_ge(w_in[n % 2], 16 * (n // 2 + 1))
                eng.activation(w_hi[:, W_ORDER[n], :, :], stage32[n % 2], ACT.Copy, scale=WS).then_inc(w_hi_done, 1)

            def take_high(step, b, big_t):
                n = step[1] % NT
                wait_full(eng, step, b)
                eng.activation(big_t[:, 0, :, n * P:(n + 1) * P], bank(step)[:, :].rearrange("p (t n) -> p t n", t=ND),
                               ACT.Copy).then_inc(in_hi, 1)

            def mid(tail, head, i, order=None):
                b = i + 1 if tail else i
                for step in order or order_mid(tail, head):
                    kind = step[0]
                    if kind == "IN":
                        take_high(step, b, fT)
                    elif kind in ("Q", "K"):
                        g, k = step[1], int(kind == "K")
                        wait_full(eng, step, b)
                        if k and g >= 1:
                            eng.wait_ge(qk_lo, b * 2 * NG + 2 * g - 1)
                        elif k and tail:
                            eng.wait_ge(qk_lo, b * 2 * NG - 1)
                        elif not k and g >= 2:
                            eng.wait_ge(qk_lo, b * 2 * NG + 2 * g - 2)
                            wait_read(eng, ("KS", g - 2), b)
                        elif not k and tail:
                            eng.wait_ge(qk_lo, i * 2 * NG + 2 * NG - 2 + 2 * g)
                            wait_read(eng, ("KS", NG - 2 + g), i)
                        eng.activation(qk32[:, 2 if k else g % 2, :], bank(step, i)[:, :], ACT.Identity,
                                       bias=(bias_k if k else bias_q)[:, g:g + 1],
                                       scale=1.0 / WS if k else SCALE / WS).then_inc(read(step, i), 1)
                    elif kind == "VS":
                        wait_full(eng, step, b)
                        eng.activation(vsT[:, step[1], :], bank(step, i)[:, :], ACT.Copy, scale=1.0 / WS
                                       ).then_inc(read(step, i), 1)
                    elif kind == "V":
                        wait_full(eng, step, b)
                        eng.activation(V[:, step[1], :], bank(step, i)[:, :], ACT.Copy, scale=1.0 / WS
                                       ).then_inc(read(step, i), 1)
                    elif kind == "SMAX":
                        _, g, u = step
                        t, q = divmod(u, 2)
                        for j in (2 * q, 2 * q + 1):
                            eng.wait_ge(max_done, b * MAXIMA + (g * 2 * NT + u) * 2 + j % 2 + 1)
                            h = NG * j + g
                            ins = eng.activation(bank(step, i)[:, j % 2, :], bank(step, i)[:, j % 2, :], ACT.Exp,
                                                 bias=nmx[:, t, h:h + 1], accum_out=esum[:, t, h:h + 1])
                        ins.then_inc(read(step, i), 1)
                    elif kind == "NEG":
                        wait_full(eng, ("SELF", NG - 1), b)
                        if tail:
                            eng.wait_ge(norms_done, b)
                        for t in range(NT):
                            op = eng.activation(self2[:, 0, t * P:(t + 1) * P], lone[3][t * DH:t * DH + H, 0:P],
                                                ACT.Copy, scale=-1.0)
                        op.then_inc(read(("SELF", 0)), NG)
                    elif kind == "SROW":
                        eng.wait_ge(self_diff, b * 2 + 2)
                        eng.activation(self2[:, :, :], self2[:, :, :], ACT.Exp).then_inc(self_exp, 1)
                    elif kind == "X2T":
                        t = step[1]
                        wait_full(eng, step, i)
                        eng.activation(x2T[:, t % 2, :], bank(step, i)[:, :], ACT.Copy).then_inc(read(step, i), 1)
                    elif kind == "HID":
                        t = step[1]
                        if t == 0:
                            eng.wait_ge(par_in, i * 96 + 96)
                        wait_full(eng, step, i)
                        eng.activation(hT[:, t % 2, :], bank(step, i)[:, 0:P], ACT.Relu, bias=b1c[:, :]
                                       ).then_inc(read(step, i), 1)
                    elif kind == "SQ":
                        t = step[1]
                        eng.wait_ge(mean_done, i * NT + t + 1)
                        eng.activation(junk[:, t % 2, :], y[:, t % 2, :], ACT.Square, bias=st[:, t % 2, 1:2],
                                       accum_out=st[:, t % 2, 2:3]).then_inc(sq_done, 1)
                    elif kind == "LOW":
                        t = step[1]
                        wait_full(eng, step, i)
                        eng.activation(lowT[:, t % 2, :], bank(step, i)[:, 0:P], ACT.Identity,
                                       bias=ident[:, RANK:RANK + 1]
                                       ).then_inc(read(step, i), 1)

            def attention(i):
                wait_free(eng, ("NORMS", 0), i)
                for n in range(NSTEP):
                    g, k = divmod(n, NT)
                    if n >= 2:
                        wait_used(eng, n - 2, i)
                    for u in range(2):
                        step = ("ST", g, k, u)
                        wait_full(eng, step, i)
                        eng.activation(big[:, n % 2, 2 * u:2 * u + 2, :], bank(step)[:, :, :], ACT.Exp
                                       ).then_inc(read(step), 1)
                wait_full(eng, ("PREPB",), i)
                eng.activation(lowB[:, :], lone[2][:, :], ACT.Copy).then_inc(read(("PREPB",)), 1)
                wait_full(eng, ("PREPA",), i)
                eng.activation(ecol[:, :], lone[3][:, 0:NT + ND * LR], ACT.Copy).then_inc(read(("PREPA",)), 1)

            def layer1(i, head, order=ORDER_L1):
                for step in order:
                    kind = step[0]
                    t = step[-1]
                    if kind == "NIN" and head:
                        take_high(step, i, xT)
                    elif kind == "X1T":
                        wait_full(eng, step, i)
                        eng.activation(q1T[:, t % 2, 0, :, :], bank(step, i)[:, :].rearrange("p (t n) -> p t n", t=ND),
                                       ACT.Copy).then_inc(q1_hi, 1)
                    elif kind == "WO":
                        wait_read(eng, ("PREPA",), i)
                        wait_read(eng, step, i)
                        if t >= 2:
                            wait_full(eng, ("X1T", t - 2), i)
                        eng.activation(q1[:, t % 2, :], x1[:, t, :], ACT.Identity, bias=ecol[:, t:t + 1]
                                       ).then_inc(q1_done, 1)
                    elif kind == "S1":
                        eng.wait_ge(max1, i * NT + t + 1)
                        if t >= 2:
                            wait_full(eng, ("P1T", t - 2), i)
                        eng.activation(p1[:, t % 2, :], bank(step, i)[:, :], ACT.Exp, bias=nmax[:, t % 2:t % 2 + 1],
                                       accum_out=rsum[:, t % 2:t % 2 + 1]).then_inc(read(step, i), 1)
                    elif kind == "P1T":
                        wait_full(eng, step, i)
                        if t >= 2:
                            wait_full(eng, ("PV1", t - 2), i)
                        eng.activation(p1T[:, t % 2, 0, :, :], bank(step, i)[:, :].rearrange("p (t n) -> p t n", t=NT),
                                       ACT.Copy, scale=PS).then_inc(p1_hi, 1)

            weight_high(0)
            for n in range(NT):
                take_high(("NIN", n), -1, xT)
            for n in range(1, 4):
                weight_high(n)
            eng.wait_ge(bias_done, 3)
            mid(False, True, 0)
            with eng.Fori(0, B - 1) as i:
                attention(i)
                layer1(i, True)
                mid(True, True, i)
            attention(B - 1)
            for step in order_last():
                if step in ADAPTER_STEPS:
                    mid(True, False, B - 1, [step])
                else:
                    layer1(B - 1, False, [step])

        @block.vector
        def _(eng):
            eng.memset(norms16[:, :, :], 0.0).then_inc(rows_ready, 1)
            eng.memset(small[:, :], 0.0).then_inc(rows_ready, 1)
            eng.memset(smallb4[:, :, :, :], 0.0).then_inc(rows_ready, 1)
            eng.wait_ge(consts, 3)
            for j in range(NJ):
                for g in range(NG):
                    eng.memset(head_cols[DH * j:DH * j + DH, g, NG * j + g:NG * j + g + 1], 1.0 / WS
                               ).then_inc(rows_ready, 1)
            eng.wait_ge(full[2], 1)
            eng.tensor_copy(cols[:, :], lone[2][:, 0:20]).then_inc(free[2], 1)
            eng.wait_ge(len_in, 16)
            eng.tensor_copy(lens_f[:, :], lens_i[:, :]).then_inc(len_cast, 1)
            eng.wait_ge(len_cast, 1)
            eng.wait_ge(sel_ready, 2 + 2 * NG)
            eng.tensor_copy(head_rows[:, :, :], head_rows32[:, :, :]).then_inc(rows_ready, 1)
            eng.tensor_scalar(mask16, kpos, lens_f[:, 0:1], -BIG, ALU.is_ge, ALU.mult).then_inc(mask_made, 1)

            def weight_low(n):
                eng.wait_ge(w_hi_done, n + 1)
                eng.scalar_tensor_tensor(out=w_lo[:, W_ORDER[n], :, :], in0=stage32[n % 2], scalar=WS,
                                         in1=w_hi[:, W_ORDER[n], :, :], op0=ALU.mult, op1=ALU.subtract
                                         ).then_inc(w_lo_done, 1)

            def bias_rows(n):
                eng.wait_ge(bias_full, n + 1)
                eng.tensor_copy(q1[0:2 - n, n, :], pair[4 + 2 * n][0:2 - n, 0, :]).then_inc(bias_row, 1)

            def biases():
                of_k = pair[4][:, 1, 0:2 * NG].rearrange("p (g v) -> p v g", v=2)
                eng.wait_ge(free[2], 1)
                eng.wait_ge(bias_full, 4)
                eng.tensor_tensor(bias_k[:, :], of_k[:, 1, :], cols[:, 4:8], ALU.add).then_inc(bias_done, 1)
                eng.tensor_tensor(t2[:, 0:4], pair[6][:, 1, 0:NG], cols[:, 0:4], ALU.add).then_inc(sums_done, 1)
                eng.tensor_tensor(t2[:, 4:8], of_k[:, 0, :], cols[:, 4:8], ALU.add).then_inc(sums_done, 1)
                eng.wait_ge(sums_done, 2)
                eng.tensor_scalar(bias_q[:, :], t2[:, 0:4], SCALE, None, ALU.mult).then_inc(bias_done, 1)
                eng.tensor_scalar(bias_ks[:, :], t2[:, 4:8], WS, None, ALU.mult).then_inc(bias_done, 1)

            def take_low(step, b, big_t, high_count):
                n = step[1] % NT
                at = slice(n * P, (n + 1) * P)
                eng.wait_ge(in_hi, high_count)
                eng.tensor_tensor(big_t[:, 1, :, at], bank(step)[:, :].rearrange("p (t n) -> p t n", t=ND),
                                  big_t[:, 0, :, at], ALU.subtract).then_inc(read(step), 1)

            def add_values(step, i):
                t = step[1]
                eng.wait_ge(rec1, i * NT + t + 1)
                wait_full(eng, step, i)
                eng.wait_ge(q1_done, i * NT + t + 1)
                eng.scalar_tensor_tensor(out=x1[:, t, :], in0=tile_of(step, i), scalar=rrec[:, t:t + 1],
                                         in1=x1[:, t, :], op0=ALU.mult, op1=ALU.add).then_inc(read(step, i), 1)

            def norm_piece(t, piece, i):
                si = st[:, :, :].bitcast(I32)
                var, r, c, c_int, r_int = st[:, :, 3], st[:, :, 4], st[:, :, 5], si[:, :, 5], si[:, :, 4]
                base = i * (NT // 2 * NEWTON) + t // 2 * NEWTON
                each = NEWTON // (NORM_PIECES - 1)
                for n in range(piece * each, min(piece * each + each, NEWTON)):
                    if n == 0:
                        eng.wait_ge(sq_done, i * NT + t + 2)
                    else:
                        eng.wait_ge(newton, base + n)
                    if n == 0:
                        op = eng.tensor_scalar(var, st[:, :, 2], 1.0 / D, EPS, ALU.mult, ALU.add)
                    elif n == 1:
                        op = eng.tensor_scalar(c_int, si[:, :, 3], 1, None, ALU.logical_shift_right)
                    elif n == 2:
                        op = eng.tensor_scalar(r_int, c_int, -1, 0x5F3759DF, ALU.mult, ALU.add)
                    elif n % 4 == 3:
                        op = eng.tensor_tensor(c, r, r, ALU.mult)
                    elif n % 4 == 0:
                        op = eng.tensor_tensor(c, c, var, ALU.mult)
                    elif n % 4 == 1:
                        op = eng.tensor_scalar(c, c, -0.5, 1.5, ALU.mult, ALU.add)
                    else:
                        op = eng.tensor_tensor(r, r, c, ALU.mult)
                    op.then_inc(newton, 1)
                if piece == NORM_PIECES - 1:
                    eng.wait_ge(newton, base + NEWTON)
                    for n in range(2):
                        eng.tensor_scalar(y[:, n, :], y[:, n, :], st[:, n, 1:2], st[:, n, 4:5], ALU.add, ALU.mult
                                          ).then_inc(normed, 1)

            def mid(tail, head, i, order=None):
                b = i + 1 if tail else i
                for step in order or order_mid(tail, head):
                    kind = step[0]
                    if kind == "IN":
                        take_low(step, b, fT, b * 2 * NT + step[1] + 1)
                    elif kind == "PV1":
                        add_values(step, i)
                    elif kind == "KS":
                        g = step[1]
                        wait_full(eng, step, b)
                        wait_read(eng, ("Q", g), b)
                        if g >= 1:
                            wait_full(eng, ("SELF", g - 1), b)
                        elif tail:
                            wait_full(eng, ("SELF", NG - 1), i)
                        eng.scalar_tensor_tensor(out=prod[:, :], in0=bank(step, i)[:, :], scalar=bias_ks[:, g:g + 1],
                                                 in1=qk32[:, g % 2, :], op0=ALU.add, op1=ALU.mult
                                                 ).then_inc(read(step, i), 1)
                    elif kind == "SMAX":
                        _, g, u = step
                        t, q = divmod(u, 2)
                        wait_full(eng, step, b)
                        for j in (2 * q, 2 * q + 1):
                            h = NG * j + g
                            eng.tensor_reduce(nmx[:, t, h:h + 1], bank(step, i)[:, j % 2, :], AX_X, ALU.max,
                                              negate=True).then_inc(max_done, 1)
                    elif kind == "MROW":
                        wait_full(eng, step, b)
                        wait_read(eng, ("SELF", NG - 1), b)
                        if tail:
                            eng.wait_ge(shift_in, b * 16)
                        eng.tensor_tensor(shift[:, :], bank(step, i)[0:H, 0, :], self2[:, 0, :], ALU.min
                                          ).then_inc(self_neg, 1)
                        eng.wait_ge(self_neg, b + 1)
                        eng.tensor_tensor(self2[:, 1, :], shift[:, :], bank(step, i)[0:H, 0, :], ALU.subtract
                                          ).then_inc(read(step, i), 1)
                        eng.tensor_tensor(self2[:, 0, :], shift[:, :], self2[:, 0, :], ALU.subtract
                                          ).then_inc(self_diff, 2)
                    elif kind == "SROW":
                        wait_full(eng, step, b)
                        eng.wait_ge(self_exp, b + 1)
                        eng.tensor_tensor(norms[:, 0, :], bank(step, i)[0:H, 0, :], self2[:, 1, :], ALU.mult
                                          ).then_inc(read(step, i), 1)
                        wait_read(eng, step, b)
                        eng.tensor_tensor(norms[:, 0, :], norms[:, 0, :], self2[:, 0, :], ALU.add).then_inc(den, 1)
                        eng.wait_ge(den, b * 2 + 1)
                        eng.reciprocal(norms[:, 0, :], norms[:, 0, :]).then_inc(den, 1)
                        if tail:
                            eng.wait_ge(stored, b * NT * 16)
                        eng.wait_ge(den, b * 2 + 2)
                        eng.tensor_tensor(norms[:, 1, :], norms[:, 0, :], self2[:, 0, :], ALU.mult
                                          ).then_inc(norms_done, 1)
                        eng.wait_ge(norms_done, b + 1)
                        eng.tensor_scalar(norms16[0:H, :, :], norms[:, :, :], RS, None, ALU.mult).then_inc(norms_hi, 1)
                        eng.wait_ge(norms_hi, b + 1)
                        eng.scalar_tensor_tensor(out=norms16[LOW_ROW:NROWS, :, :], in0=norms[:, :, :], scalar=RS,
                                                 in1=norms16[0:H, :, :], op0=ALU.mult, op1=ALU.subtract
                                                 ).then_inc(norms_lo, 1)
                    elif kind == "ADP":
                        t = step[1]
                        wait_full(eng, step, i)
                        eng.wait_ge(xb_done, i * NT + t + 1)
                        if t >= 2:
                            eng.wait_ge(x3_done, i * NT + t - 1)
                        eng.scalar_tensor_tensor(out=y[:, t % 2, :], in0=bank(step, i)[:, :], scalar=1.0,
                                                 in1=xb[:, t % 2, :], op0=ALU.mult, op1=ALU.add,
                                                 accum_out=st[:, t % 2, 0:1]).then_inc(read(step, i), 1)
                        wait_read(eng, step, i)
                        eng.tensor_scalar(st[:, t % 2, 1:2], st[:, t % 2, 0:1], -1.0 / D, None, ALU.mult
                                          ).then_inc(mean_done, 1)
                    elif kind == "NORM":
                        norm_piece(step[1], step[2], i)
                    elif kind == "X3T":
                        t = step[1]
                        wait_full(eng, step, i)
                        eng.tensor_copy(x3T[:, t % 2, :], bank(step, i)[:, :]).then_inc(read(step, i), 1)
                    elif kind == "LORA":
                        t = step[1]
                        wait_full(eng, step, i)
                        eng.tensor_tensor(x1[:, t, :], bank(step, i)[:, :], x1[:, t, :], ALU.add
                                          ).then_inc(read(step, i), 1)

            def take_norms(g, i):
                wait_full(eng, ("NORMS", g), i)
                eng.tensor_copy(spread[:, g, :], lone[2][:, :]).then_inc(read(("NORMS", g)), 1)
                wait_full(eng, ("SELFW", g), i)
                wait_read(eng, ("VS", g), i)
                eng.tensor_tensor(vsT[:, g, :], lone[3][:, :], vsT[:, g, :], ALU.mult
                                  ).then_inc(read(("SELFW", g)), 1)

            def finish_group(g, i):
                wait_full(eng, ("PV", g), i)
                wait_read(eng, ("NORMS", g), i)
                eng.tensor_tensor(t1[:, :], bank(("PV", g))[:, :], spread[:, g, :], ALU.mult
                                  ).then_inc(read(("PV", g)), 1)
                wait_read(eng, ("PV", g), i)
                wait_read(eng, ("SELFW", g), i)
                eng.tensor_tensor(t2[:, :], t1[:, :], vsT[:, g, :], ALU.add).then_inc(att_f32, 1)
                eng.wait_ge(att_f32, i * NG + g + 1)
                eng.tensor_scalar(aT[:, 0, g, :], t2[:, :], cols[:, 8 + g:9 + g], None, ALU.add).then_inc(att_hi, 1)
                eng.wait_ge(att_hi, i * NG + g + 1)
                eng.scalar_tensor_tensor(out=aT[:, 1, g, :], in0=t2[:, :], scalar=cols[:, 8 + g:9 + g],
                                         in1=aT[:, 0, g, :], op0=ALU.add, op1=ALU.subtract).then_inc(att_lo, 1)

            def attention(i):
                eng.wait_ge(prep_in, i * 48 + 48)
                for c in range(ND):
                    eng.tensor_copy(smallb4[:, :, c, 0:RANK], smallb[:, :, :]).then_inc(copied, 1)
                take_norms(0, i)
                finish_group(0, i)
                for g in range(1, NG):
                    take_norms(g, i)
                for g in range(1, NG):
                    finish_group(g, i)

            def layer1(i, head, order=ORDER_L1):
                for step in order:
                    kind, t = step[0], step[-1]
                    if kind == "NIN" and head:
                        take_low(step, i, xT, i * 2 * NT + (2 * NT + t + 1))
                    elif kind == "WO":
                        eng.wait_ge(x_bo, i * NT + t + 1)
                        wait_full(eng, step, i)
                        eng.scalar_tensor_tensor(out=x1[:, t, :], in0=bank(step, i)[:, t % 2, :], scalar=1.0 / WS,
                                                 in1=x1[:, t, :], op0=ALU.mult, op1=ALU.add
                                                 ).then_inc(read(step, i), 1)
                    elif kind == "X1T":
                        eng.wait_ge(q1_hi, i * NT + t + 1)
                        eng.tensor_tensor(q1T[:, t % 2, 1, :, :], bank(step, i)[:, :].rearrange("p (t n) -> p t n", t=ND),
                                          q1T[:, t % 2, 0, :, :], ALU.subtract).then_inc(read(step, i), 1)
                    elif kind == "S1":
                        wait_full(eng, step, i)
                        if t >= 2:
                            wait_read(eng, ("S1", t - 2), i)
                        eng.tensor_reduce(nmax[:, t % 2:t % 2 + 1], bank(step, i)[:, :], AX_X, ALU.max,
                                          negate=True).then_inc(max1, 1)
                    elif kind == "P1T":
                        wait_read(eng, ("S1", t), i)
                        eng.tensor_scalar(rrec[:, t:t + 1], rsum[:, t % 2:t % 2 + 1], PS, None, ALU.mult
                                          ).then_inc(sum1, 1)
                        eng.wait_ge(sum1, i * NT + t + 1)
                        eng.reciprocal(rrec[:, t:t + 1], rrec[:, t:t + 1]).then_inc(rec1, 1)
                        eng.wait_ge(p1_hi, i * NT + t + 1)
                        eng.scalar_tensor_tensor(out=p1T[:, t % 2, 1, :, :],
                                                 in0=bank(step, i)[:, :].rearrange("p (t n) -> p t n", t=NT), scalar=PS,
                                                 in1=p1T[:, t % 2, 0, :, :], op0=ALU.mult, op1=ALU.subtract
                                                 ).then_inc(read(step, i), 1)
                    elif kind == "PV1":
                        add_values(step, i)

            weight_low(0)
            bias_rows(0)
            for n in range(NT):
                take_low(("NIN", n), -1, xT, n + 1)
            weight_low(1)
            bias_rows(1)
            biases()
            for n in (2, 3):
                weight_low(n)
            eng.wait_ge(bias_done, 3)
            eng.wait_ge(mask_out, 16)
            mid(False, True, 0)
            with eng.Fori(0, B - 1) as i:
                attention(i)
                layer1(i, True)
                mid(True, True, i)
            attention(B - 1)
            for step in order_last():
                if step in ADAPTER_STEPS:
                    mid(True, False, B - 1, [step])
                else:
                    layer1(B - 1, False, [step])

        @block.tensor
        def _(eng):
            eng.wait_ge(sel_ready, 1)
            eng.wait_ge(vec_in, 5 * 16)
            eng.transpose(lone[2][:, 0:20], vecs[:, :], ident[0:20, 0:20]).then_inc(full[2], 1)

            def vector_rows(n):
                eng.wait_ge(w_in[n], 16)
                for d in range(ND):
                    mm = eng.matmul(pair[4 + 2 * n][0:2 - n, 0, :], cols[:, 12 + d:(17 if n == 0 else 13) + d:4],
                                    stage32[n][:, d, :], start=(d == 0), stop=(d == ND - 1))
                mm.then_inc(bias_full, 1)

            def vector_cols(n):
                eng.wait_ge(bias_row, n + 1)
                m = 2 - n
                for g in range(NG):
                    mm = eng.transpose(pair[4 + 2 * n][:, 1, m * g:m * g + m], q1[0:m, n, g * P:(g + 1) * P],
                                       ident[0:m, 0:m])
                mm.then_inc(bias_full, 1)

            def weights(w, d, n):
                at = slice(n * P, (n + 1) * P)
                return w_hi[:, w, d, at], w_lo[:, w, d, at]

            def transpose4(step, src, b):
                for d in range(4):
                    mm = eng.transpose(bank(step, b)[:, d * P:(d + 1) * P], src[:, d * P:(d + 1) * P], ident[:, :])
                mm.then_inc(done(step, b), 1)

            def weigh_values(step, i):
                t = step[1]
                if t == 0:
                    eng.wait_ge(f_lo, i * NT + NT)
                wait_read(eng, ("P1T", t), i)
                wait_free(eng, step, i)
                hi_lo(eng, tile_of(step, i), [(p1T[:, t % 2, 0, k, :], p1T[:, t % 2, 1, k, :]) for k in range(NT)],
                      [(f16[:, 0, k, :], f16[:, 1, k, :]) for k in range(NT)]).then_inc(done(step, i), 1)

            def project(step, part, b):
                kind, g = step
                if part == 0:
                    if step == ("VS", 0) and isinstance(b, int):
                        eng.wait_ge(w_lo_done, 4)
                    if step == ("Q", 0):
                        wait_read(eng, ("IN", 2 * NT - 2), b)
                        wait_read(eng, ("IN", 2 * NT - 1), b)
                    wait_free(eng, step, b)
                if kind == "V":
                    at = slice(g * P, (g + 1) * P)
                    left = [(xT[:, 0, d, at], xT[:, 1, d, at]) for d in range(ND)]
                    right = [(w_hi[:, 2, d, :], w_lo[:, 2, d, :]) for d in range(ND)]
                else:
                    src = xT if kind == "K" else fT
                    left = [weights({"Q": 0, "K": 1, "KS": 1, "VS": 2}[kind], d, g) for d in range(ND)]
                    right = [(src[:, 0, d, :], src[:, 1, d, :]) for d in range(ND)]
                return hi_lo(eng, bank(step)[:, :], left, right, part=part)

            def mid(tail, head, i, order=None):
                b = i + 1 if tail else i
                for step in order or order_mid(tail, head):
                    kind = step[0]
                    if kind == "IN":
                        n = step[1] - NT
                        eng.wait_ge(tile_in[n], b * 32 + 32)
                        wait_free(eng, step, b)
                        transpose4(step, tiles_in[:, n, :], i)
                    elif kind == "PART":
                        project(step[2], step[1], b)
                    elif kind in ("Q", "K", "KS", "VS", "V"):
                        project(step, PARTS - 1, b).then_inc(done(step, i), 1)
                    elif kind == "SELF":
                        g = step[1]
                        if g == 0 and not tail:
                            eng.wait_ge(rows_ready, 4 + H)
                        if g == 0:
                            wait_free(eng, step, b)
                        wait_read(eng, ("KS", g), b)
                        for t in range(NT):
                            mm = eng.matmul(lone[3][t * DH:t * DH + H, 0:P], head_cols[:, g, :],
                                            prod[:, t * P:(t + 1) * P], start=(g == 0), stop=(g == NG - 1),
                                            skip_group_check=True)
                        mm.then_inc(done(step, i), 1)
                    elif kind == "SMAX":
                        _, g, u = step
                        t, q = divmod(u, 2)
                        if u == 0:
                            eng.wait_ge(stacked[g], b * DMAS_PER_STACK + DMAS_PER_STACK)
                            if g == 0:
                                eng.wait_ge(mask_in, b * 16 + 16)
                        wait_free(eng, step, b)
                        for j in (2 * q, 2 * q + 1):
                            mm = eng.matmul(bank(step, i)[:, j % 2, :], KQ[0:SHIFT_ROW, j, g, 1, t * P:(t + 1) * P],
                                            KQ[0:SHIFT_ROW, j, g, 0, :], start=True, stop=True)
                        mm.then_inc(done(step, i), 1)
                    elif kind == "MROW":
                        eng.wait_ge(max_done, b * MAXIMA + MAXIMA)
                        wait_free(eng, step, b)
                        for t in range(NT):
                            mm = eng.transpose(bank(step, i)[0:H, 0, t * P:(t + 1) * P], nmx[:, t, :], ident[:, :])
                        mm.then_inc(done(step, i), 1)
                    elif kind == "SROW":
                        wait_read(eng, ("SMAX", NG - 1, 2 * NT - 2), b)
                        wait_read(eng, ("SMAX", NG - 1, 2 * NT - 1), b)
                        wait_free(eng, step, b)
                        for t in range(NT):
                            mm = eng.transpose(bank(step, i)[0:H, 0, t * P:(t + 1) * P], esum[:, t, :], ident[:, :])
                        mm.then_inc(done(step, i), 1)
                    elif kind == "X2T":
                        t = step[1]
                        wait_read(eng, ("PV1", t), i)
                        wait_free(eng, step, i)
                        transpose4(step, x1[:, t, :], i)
                    elif kind == "HID":
                        t = step[1]
                        if t == 0:
                            eng.wait_ge(par_in, i * 96 + 96)
                        wait_free(eng, step, i)
                        for d in range(ND):
                            mm = eng.matmul(bank(step, i)[:, 0:P], w1[:, d, :], x2T[:, t % 2, d * P:(d + 1) * P],
                                            start=(d == 0), stop=(d == ND - 1))
                        mm.then_inc(done(step, i), 1)
                    elif kind == "ADP":
                        wait_free(eng, step, i)
                        eng.matmul(bank(step, i)[:, :], hT[:, step[1] % 2, :], w2[:, :], start=True, stop=True
                                   ).then_inc(done(step, i), 1)
                    elif kind == "PV1":
                        weigh_values(step, i)
                    elif kind == "X3T":
                        t = step[1]
                        eng.wait_ge(x3_done, i * NT + t + 1)
                        wait_free(eng, step, i)
                        transpose4(step, x1[:, t, :], i)
                    elif kind == "LOW":
                        t = step[1]
                        wait_free(eng, step, i)
                        for d in range(ND):
                            mm = eng.matmul(bank(step, i)[d * LR:(d + 1) * LR, 0:P],
                                            ecol[:, NT + d * LR:NT + (d + 1) * LR],
                                            x3T[:, t % 2, d * P:(d + 1) * P], start=True, stop=True,
                                            skip_group_check=True)
                        mm.then_inc(done(step, i), 1)
                    elif kind == "LORA":
                        if step[1] == 0:
                            eng.wait_ge(emb_in, i * 16 + 16)
                        wait_free(eng, step, i)
                        eng.matmul(bank(step, i)[:, :], lowT[:, step[1] % 2, :], lowB[:, :], start=True, stop=True
                                   ).then_inc(done(step, i), 1)

            def scores(n, i):
                g, k = divmod(n, NT)
                for u in range(2):
                    step = ("ST", g, k, u)
                    wait_free(eng, step, i)
                    for j in (2 * u, 2 * u + 1):
                        mm = eng.matmul(bank(step)[:, j % 2, :], KQ[0:SHIFT_ROW + 1, j, g, 0, k * P:(k + 1) * P],
                                        KQ[0:SHIFT_ROW + 1, j, g, 1, :], start=True, stop=True)
                    mm.then_inc(done(step), 1)

            def values(n, i):
                g, k = divmod(n, NT)
                if k == 0:
                    wait_free(eng, ("PV", g), i)
                if g == 0:
                    wait_read(eng, ("V", k), i)
                for u in range(2):
                    wait_read(eng, ("ST", g, k, u), i)
                for j in range(NJ):
                    q = slice(j * DH, (j + 1) * DH)
                    mm = eng.matmul(bank(("PV", g))[q, :], V[:, k, g * P + j * DH:g * P + (j + 1) * DH],
                                    big[:, n % 2, j, :], start=(k == 0), stop=(k == NT - 1), skip_group_check=True)
                mm.then_inc(pv_done if k < NT - 1 else done(("PV", g)), 1)

            def spread_norms(g, i):
                if g == 0:
                    eng.wait_ge(norms_lo, i + 1)
                for n, name in enumerate(("NORMS", "SELFW")):
                    wait_free(eng, (name, g), i)
                    eng.matmul(lone[2 + n][:, :], head_rows[:, g, :], norms16[:, n, :], start=True, stop=True
                               ).then_inc(done((name, g)), 1)

            def small_tables(i):
                eng.wait_ge(copied, i * ND + ND)
                wait_free(eng, ("PREPA",), i)
                wait_free(eng, ("PREPB",), i)
                for d in range(ND):
                    mm = eng.transpose(lone[2][:, d * P:(d + 1) * P],
                                       smallb4[:, d, :, :].rearrange("p c r -> p (c r)"), ident[:, :])
                mm.then_inc(done(("PREPB",)), 1)
                eng.transpose(lone[3][:, 0:NT], erow[:, :], ident[0:NT, 0:NT])
                for d in range(ND):
                    mm = eng.transpose(lone[3][:, NT + d * LR:NT + (d + 1) * LR],
                                       small[:, d * P:(d + 1) * P], ident[0:LR, 0:LR])
                mm.then_inc(done(("PREPA",)), 1)

            def attention(i):
                eng.wait_ge(shift_in, i * 16 + 16)
                scores(0, i)
                for n in range(NSTEP):
                    if n + 1 < NSTEP:
                        scores(n + 1, i)
                    else:
                        layer1(i, False, [("WOP", 0)])
                    values(n, i)
                    if n in NORMS_AT:
                        spread_norms(NORMS_AT.index(n), i)
                    if n == NSTEP - 3:
                        small_tables(i)

            def next_x(step, i):
                n = step[1]
                eng.wait_ge(tile_in[n], i * 32 + 48)
                wait_free(eng, step, i)
                transpose4(step, tiles_in[:, n, :], i)

            def layer1(i, head, order=ORDER_L1):
                for step in order:
                    kind, t = step[0], step[-1]
                    if kind == "NIN" and head:
                        next_x(step, i)
                    elif kind == "WOP":
                        at = slice(t * P, (t + 1) * P)
                        if t == 0:
                            eng.wait_ge(att_lo, i * NG + NG - 1)
                        wait_free(eng, ("WO", t - t % 2), i)
                        hi_lo(eng, bank(("WO", t))[:, t % 2, :],
                              [(aT[:, 0, g, at], aT[:, 1, g, at]) for g in range(NG - 1)],
                              [(w_hi[:, 3, g, :], w_lo[:, 3, g, :]) for g in range(NG - 1)], last=False)
                    elif kind == "WO":
                        g, at = NG - 1, slice(t * P, (t + 1) * P)
                        if t == 0:
                            eng.wait_ge(att_lo, i * NG + NG)
                        hi_lo(eng, bank(step, i)[:, t % 2, :], [(aT[:, 0, g, at], aT[:, 1, g, at])],
                              [(w_hi[:, 3, g, :], w_lo[:, 3, g, :])], first=False).then_inc(done(step, i), 1)
                    elif kind == "X1T":
                        eng.wait_ge(q1_done, i * NT + t + 1)
                        wait_free(eng, step, i)
                        transpose4(step, q1[:, t % 2, :], i)
                    elif kind == "S1":
                        wait_read(eng, ("X1T", t), i)
                        wait_free(eng, step, i)
                        hi_lo(eng, bank(step, i)[:, :],
                              [(q1T[:, t % 2, 0, d, :], q1T[:, t % 2, 1, d, :]) for d in range(ND)],
                              [(fT[:, 0, d, :], fT[:, 1, d, :]) for d in range(ND)]).then_inc(done(step, i), 1)
                    elif kind == "P1T":
                        wait_read(eng, ("S1", t), i)
                        wait_free(eng, step, i)
                        transpose4(step, p1[:, t % 2, :], i)
                    elif kind == "PV1":
                        weigh_values(step, i)

            eng.wait_ge(free[2], 1)
            vector_rows(0)
            for n in range(NT):
                next_x(("NIN", n), -1)
            vector_rows(1)
            vector_cols(0)
            vector_cols(1)
            eng.wait_ge(w_lo_done, 2)
            mid(False, True, 0)
            with eng.Fori(0, B - 1) as i:
                attention(i)
                layer1(i, True)
                mid(True, True, i)
            attention(B - 1)
            for step in order_last():
                if step in ADAPTER_STEPS:
                    mid(True, False, B - 1, [step])
                else:
                    layer1(B - 1, False, [step])


_INS = ['x', 'fside_BxSxS_0', 'itok_B_18_1004', 'itok_B_0_5', 'itok_B_0_8', 'itok_B_0_3',
        'L0_cond_Wq', 'L0_cond_bq', 'L0_cond_Wk', 'L0_cond_bk', 'L0_cond_Wv', 'L0_cond_bv', 'L0_cond_Wo',
        'L0_cond_bo', 'L0_cond_b_prev', 'L0_cond_b_self', 'L1_cond_braak_embed', 'L2_cond_W1', 'L2_cond_b1',
        'L2_cond_W2', 'L2_cond_b2', 'L2_cond_gamma', 'L2_cond_beta', 'L3_cond_lora_A', 'L3_cond_lora_B',
        'L3_cond_lang_embed']
_OUTS = [((B, S, D), 'float32')]


def kernel(**inputs):
    import numpy as _np
    import concourse.bacc as _bacc
    from concourse import mybir as _mybir
    from concourse.bass_utils import run_bass_kernel_spmd as _run

    nc = _bacc.Bacc("TRN2", target_bir_lowering=False, num_devices=1)
    arrays, args = {}, []
    for name in _INS:
        a = _np.ascontiguousarray(inputs[name])
        arrays[f"in_{name}_dram"] = a
        args.append(nc.dram_tensor(f"in_{name}_dram", a.shape, _mybir.dt.from_np(a.dtype), kind="ExternalInput").ap())
    for n, (shape, dtype) in enumerate(_OUTS):
        dt = _mybir.dt.from_np(_np.dtype(dtype))
        args.append(nc.dram_tensor(f"out_{n}_dram", shape, dt, kind="ExternalOutput").ap())
    build_program(nc, *args)
    r = _run(nc, [arrays], core_ids=[0])
    got = tuple(r.results[0][f"out_{n}_dram"] for n in range(len(_OUTS)))
    return got[0]
```
